# Optimizing a Trainium2 kernel written in Bass

```python
import numpy as np
import jax
import jax.numpy as jnp

def _softmax(x, axis=-1):
    return jax.nn.softmax(x, axis=axis)

def _gelu(x):
    return jax.nn.gelu(x, approximate=True)

def _silu(x):
    return jax.nn.silu(x)

def _sigmoid(x):
    return jax.nn.sigmoid(x)

def _layernorm(x, axis=-1, eps=1e-05):
    m = jnp.mean(x, axis=axis, keepdims=True)
    v = jnp.var(x, axis=axis, keepdims=True)
    return (x - m) / jnp.sqrt(v + eps)

def _scatter_add(tgt, idx, src, axis=0):
    return tgt.at[idx].add(src)

def _segment_sum(src, seg, n):
    return jax.ops.segment_sum(src, seg, n)
kernel_name = 'mk_gnn_preln_d4_gnn_r16_dd95eb'

def setup_inputs(seed: int=0):
    np.random.seed(seed)
    _w = jnp.asarray

    def _rec_inputs():
        import jax
        import jax.numpy as jnp
        _gk = jax.random.key(seed)
        x = -0.0003713 + 1 * jax.random.normal(jax.random.fold_in(_gk, 1), (3125, 128), jnp.float32)
        _s = jax.random.randint(jax.random.fold_in(_gk, 2), (50000,), 0, 3125, jnp.int32)
        _d = jax.random.randint(jax.random.fold_in(_gk, 3), (50000,), 0, 3125, jnp.int32)
        _loop = jnp.arange(3125, dtype=jnp.int32)
        src = jnp.concatenate([_s, _d, _loop])
        dst = jnp.concatenate([_d, _s, _loop])
        _o = jnp.argsort(dst, stable=True)
        src = src[_o]
        dst = dst[_o]
        edge_type_474 = jax.random.randint(jax.random.fold_in(_gk, 13), (103125,), 0, 474, jnp.int32)
        edge_type_64 = jax.random.randint(jax.random.fold_in(_gk, 14), (103125,), 0, 64, jnp.int32)
        return (x, src, dst, edge_type_474, edge_type_64)
    x, src, dst, edge_type_474, edge_type_64 = _rec_inputs()

    def _L0_gnn_setup():
        import jax, jax.numpy as jnp
        import numpy as np
        N_HOPS = 3
        N_ENTITIES = 6250
        EMB = 128
        N_EDGES = 37500
        N_REL = 64
        key = jax.random.key(seed)
        k1, k2, k3, k4, k5, k6 = jax.random.split(key, 6)
        entity_emb = jax.random.normal(k1, (N_ENTITIES, EMB), dtype=jnp.float32)
        edge_emb = jax.random.normal(k2, (N_REL, EMB), dtype=jnp.float32)
        q_w = jax.random.normal(k3, (EMB, EMB), dtype=jnp.float32) * (1.0 / np.sqrt(EMB))
        k_w = jax.random.normal(k4, (EMB, EMB), dtype=jnp.float32) * (1.0 / np.sqrt(EMB))
        edge_index = jax.random.randint(k5, (2, N_EDGES), 0, N_ENTITIES, dtype=jnp.int64)
        edge_type = jax.random.randint(k6, (N_EDGES,), 0, N_REL, dtype=jnp.int64)
        return {'entity_emb': entity_emb, 'edge_emb': edge_emb, 'q_w': q_w, 'k_w': k_w, 'edge_index': edge_index, 'edge_type': edge_type, 'mess_dropout': 0}
    _L0_gnn_all = _L0_gnn_setup()
    _L0_gnn_in = {k: v for k, v in _L0_gnn_all.items() if k in ('edge_emb', 'q_w', 'k_w')}
    del _L0_gnn_all

    def _L1_gnn_setup():
        import jax, jax.numpy as jnp
        import numpy as np
        NEG_SLOPE = 0.2
        EPS = 1e-16
        N_NODES = 6250
        N_EDGES = 100000
        D = 128
        H = 4
        C = 32
        L = 3

        def _gat_layer(h, src, dst, Ws, Wd, a_s, a_d, bias):
            N = h.shape[0]
            xs = (h @ Ws).reshape(N, H, C)
            xd = (h @ Wd).reshape(N, H, C)
            alpha_s = jnp.sum(xs * a_s, axis=-1)
            alpha_d = jnp.sum(xd * a_d, axis=-1)
            e = alpha_s[src] + alpha_d[dst]
            e = jax.nn.leaky_relu(e, NEG_SLOPE)
            emax = jax.ops.segment_max(e, dst, num_segments=N)
            ex = jnp.exp(e - emax[dst])
            denom = jax.ops.segment_sum(ex, dst, num_segments=N)
            alpha = ex / (denom[dst] + EPS)
            msg = xs[src] * alpha[:, :, None]
            out = jax.ops.segment_sum(msg, dst, num_segments=N)
            return out.reshape(N, H * C) + bias
        key = jax.random.key(seed)
        ks = jax.random.split(key, 7)
        x = jax.random.normal(ks[0], (N_NODES, D), dtype=jnp.float32)
        edge_index = jax.random.randint(ks[1], (2, N_EDGES), 0, N_NODES, dtype=jnp.int32)
        scale = 1.0 / np.sqrt(D)
        Ws = jax.random.normal(ks[2], (L, D, H * C), dtype=jnp.float32) * scale
        Wd = jax.random.normal(ks[3], (L, D, H * C), dtype=jnp.float32) * scale
        att_s = jax.random.normal(ks[4], (L, H, C), dtype=jnp.float32) * scale
        att_d = jax.random.normal(ks[5], (L, H, C), dtype=jnp.float32) * scale
        b = jnp.zeros((L, H * C), dtype=jnp.float32)
        return {'x': x, 'edge_index': edge_index, 'Ws': Ws, 'Wd': Wd, 'att_s': att_s, 'att_d': att_d, 'b': b}
    _L1_gnn_all = _L1_gnn_setup()
    _L1_gnn_in = {k: v for k, v in _L1_gnn_all.items() if k in ('Ws', 'Wd', 'att_s', 'att_d', 'b')}
    del _L1_gnn_all

    def _L2_gnn_setup():
        import jax, jax.numpy as jnp
        import numpy as np
        N_NODES = 6250
        N_EDGES = 37500

        def _deg_norm(idx, n):
            deg = jax.ops.segment_sum(jnp.ones(idx.shape[0], jnp.float32), idx, num_segments=n)
            return jnp.where(deg > 0, deg ** (-0.5), 0.0)

        def gcn_conv(feat, src, dst, W, b):
            n = feat.shape[0]
            norm_src = _deg_norm(src, n)
            norm_dst = _deg_norm(dst, n)
            h = feat * norm_src[:, None]
            if W.shape[0] > W.shape[1]:
                h = h @ W
                agg = jax.ops.segment_sum(h[src], dst, num_segments=n)
            else:
                agg = jax.ops.segment_sum(h[src], dst, num_segments=n)
                agg = agg @ W
            return jax.nn.relu(agg * norm_dst[:, None] + b)
        key = jax.random.key(seed)
        ks = jax.random.split(key, 8)
        d_in, d_hid, d_enc, d_out = (128, 256, 128, 128)
        feat = jax.random.normal(ks[0], (N_NODES, d_in), jnp.float32)
        src = jax.random.randint(ks[1], (N_EDGES,), 0, N_NODES, jnp.int32)
        dst = jax.random.randint(ks[2], (N_EDGES,), 0, N_NODES, jnp.int32)
        W1 = jax.random.normal(ks[3], (d_in, d_hid), jnp.float32) * (1.0 / np.sqrt(d_in))
        b1 = jnp.zeros((d_hid,), jnp.float32)
        W2 = jax.random.normal(ks[4], (d_hid, d_enc), jnp.float32) * (1.0 / np.sqrt(d_hid))
        b2 = jnp.zeros((d_enc,), jnp.float32)
        fc1_w = jax.random.normal(ks[5], (d_enc, d_out), jnp.float32) * (1.0 / np.sqrt(d_enc))
        fc1_b = jnp.zeros((d_out,), jnp.float32)
        fc2_w = jax.random.normal(ks[6], (d_out, d_out), jnp.float32) * (1.0 / np.sqrt(d_out))
        fc2_b = jnp.zeros((d_out,), jnp.float32)
        return {'feat': feat, 'src': src, 'dst': dst, 'W1': W1, 'b1': b1, 'W2': W2, 'b2': b2, 'fc1_w': fc1_w, 'fc1_b': fc1_b, 'fc2_w': fc2_w, 'fc2_b': fc2_b}
    _L2_gnn_all = _L2_gnn_setup()
    _L2_gnn_in = {k: v for k, v in _L2_gnn_all.items() if k in ('W1', 'b1', 'W2', 'b2', 'fc1_w', 'fc1_b', 'fc2_w', 'fc2_b')}
    del _L2_gnn_all

    def _L3_gnn_setup():
        import jax, jax.numpy as jnp
        import numpy as np
        N_ENT = 3125
        N_EDGE = 31250
        H_DIM = 128
        N_REL = 237
        key = jax.random.key(seed)
        k1, k2, k3, k4, k5, k6 = jax.random.split(key, 6)
        ent_emb = jax.random.normal(k1, (N_ENT, H_DIM), dtype=jnp.float32)
        rel_emb = jax.random.normal(k2, (2 * N_REL, H_DIM), dtype=jnp.float32)
        neigh_w = jax.random.normal(k3, (H_DIM, H_DIM), dtype=jnp.float32) * (1.0 / np.sqrt(H_DIM))
        src = jax.random.randint(k4, (N_EDGE,), 0, N_ENT, dtype=jnp.int32)
        dst = jax.random.randint(k5, (N_EDGE,), 0, N_ENT, dtype=jnp.int32)
        rel_id = jax.random.randint(k6, (N_EDGE,), 0, 2 * N_REL, dtype=jnp.int32)
        return {'ent_emb': ent_emb, 'rel_emb': rel_emb, 'neigh_w': neigh_w, 'src': src, 'dst': dst, 'rel_id': rel_id}
    _L3_gnn_all = _L3_gnn_setup()
    _L3_gnn_in = {k: v for k, v in _L3_gnn_all.items() if k in ('rel_emb', 'neigh_w')}
    del _L3_gnn_all
    return {'x': x, 'src': src, 'dst': dst, 'edge_type_474': edge_type_474, 'edge_type_64': edge_type_64, 'L0_gnn_edge_emb': _L0_gnn_in['edge_emb'], 'L0_gnn_q_w': _L0_gnn_in['q_w'], 'L0_gnn_k_w': _L0_gnn_in['k_w'], 'L1_gnn_Ws': _L1_gnn_in['Ws'], 'L1_gnn_Wd': _L1_gnn_in['Wd'], 'L1_gnn_att_s': _L1_gnn_in['att_s'], 'L1_gnn_att_d': _L1_gnn_in['att_d'], 'L1_gnn_b': _L1_gnn_in['b'], 'L2_gnn_W1': _L2_gnn_in['W1'], 'L2_gnn_b1': _L2_gnn_in['b1'], 'L2_gnn_W2': _L2_gnn_in['W2'], 'L2_gnn_b2': _L2_gnn_in['b2'], 'L2_gnn_fc1_w': _L2_gnn_in['fc1_w'], 'L2_gnn_fc1_b': _L2_gnn_in['fc1_b'], 'L2_gnn_fc2_w': _L2_gnn_in['fc2_w'], 'L2_gnn_fc2_b': _L2_gnn_in['fc2_b'], 'L3_gnn_rel_emb': _L3_gnn_in['rel_emb'], 'L3_gnn_neigh_w': _L3_gnn_in['neigh_w']}

def reference(x, src, dst, edge_type_474, edge_type_64, L0_gnn_edge_emb, L0_gnn_q_w, L0_gnn_k_w, L1_gnn_Ws, L1_gnn_Wd, L1_gnn_att_s, L1_gnn_att_d, L1_gnn_b, L2_gnn_W1, L2_gnn_b1, L2_gnn_W2, L2_gnn_b2, L2_gnn_fc1_w, L2_gnn_fc1_b, L2_gnn_fc2_w, L2_gnn_fc2_b, L3_gnn_rel_emb, L3_gnn_neigh_w):
    import jax
    import jax.numpy as jnp

    def _L0_gnn_ref(entity_emb, edge_emb, q_w, k_w, edge_index, edge_type, mess_dropout):
        import jax, jax.numpy as jnp
        import numpy as np
        N_HOPS = 3
        N_ENTITIES = 6250
        EMB = 128
        N_EDGES = 37500
        N_REL = 64
        head = edge_index[0]
        tail = edge_index[1]
        rel = edge_emb[edge_type]
        n = entity_emb.shape[0]
        agg = entity_emb
        out = jnp.zeros_like(entity_emb)
        for _ in range(N_HOPS):
            h = agg[head]
            t = agg[tail]
            left = h @ q_w
            right = jnp.tanh(rel * t @ k_w)
            att = jnp.sum(left * right, axis=1)
            seg_max = jax.ops.segment_max(att, head, num_segments=n)
            e = jnp.exp(att - seg_max[head])
            seg_sum = jax.ops.segment_sum(e, head, num_segments=n)
            w = e / seg_sum[head]
            msg = w[:, None] * rel * t
            summed = jax.ops.segment_sum(msg, head, num_segments=n)
            cnt = jax.ops.segment_sum(jnp.ones_like(att), head, num_segments=n)
            agg = summed / jnp.maximum(cnt, 1.0)[:, None]
            norm = jnp.linalg.norm(agg, axis=1, keepdims=True)
            agg = agg / jnp.maximum(norm, 1e-12)
            out = out + agg + entity_emb
        return out

    def _L1_gnn_ref(x, edge_index, Ws, Wd, att_s, att_d, b):
        import jax, jax.numpy as jnp
        import numpy as np
        NEG_SLOPE = 0.2
        EPS = 1e-16
        N_NODES = 6250
        N_EDGES = 100000
        D = 128
        H = 4
        C = 32
        L = 3

        def _gat_layer(h, src, dst, Ws, Wd, a_s, a_d, bias):
            N = h.shape[0]
            xs = (h @ Ws).reshape(N, H, C)
            xd = (h @ Wd).reshape(N, H, C)
            alpha_s = jnp.sum(xs * a_s, axis=-1)
            alpha_d = jnp.sum(xd * a_d, axis=-1)
            e = alpha_s[src] + alpha_d[dst]
            e = jax.nn.leaky_relu(e, NEG_SLOPE)
            emax = jax.ops.segment_max(e, dst, num_segments=N)
            ex = jnp.exp(e - emax[dst])
            denom = jax.ops.segment_sum(ex, dst, num_segments=N)
            alpha = ex / (denom[dst] + EPS)
            msg = xs[src] * alpha[:, :, None]
            out = jax.ops.segment_sum(msg, dst, num_segments=N)
            return out.reshape(N, H * C) + bias
        src = edge_index[0]
        dst = edge_index[1]
        h = x
        for i in range(L):
            h = _gat_layer(h, src, dst, Ws[i], Wd[i], att_s[i], att_d[i], b[i])
            if i < L - 1:
                h = jax.nn.relu(h)
        return h

    def _L2_gnn_ref(feat, src, dst, W1, b1, W2, b2, fc1_w, fc1_b, fc2_w, fc2_b):
        import jax, jax.numpy as jnp
        import numpy as np
        N_NODES = 6250
        N_EDGES = 37500

        def _deg_norm(idx, n):
            deg = jax.ops.segment_sum(jnp.ones(idx.shape[0], jnp.float32), idx, num_segments=n)
            return jnp.where(deg > 0, deg ** (-0.5), 0.0)

        def gcn_conv(feat, src, dst, W, b):
            n = feat.shape[0]
            norm_src = _deg_norm(src, n)
            norm_dst = _deg_norm(dst, n)
            h = feat * norm_src[:, None]
            if W.shape[0] > W.shape[1]:
                h = h @ W
                agg = jax.ops.segment_sum(h[src], dst, num_segments=n)
            else:
                agg = jax.ops.segment_sum(h[src], dst, num_segments=n)
                agg = agg @ W
            return jax.nn.relu(agg * norm_dst[:, None] + b)
        h = gcn_conv(feat, src, dst, W1, b1)
        h = gcn_conv(h, src, dst, W2, b2)
        z = jax.nn.elu(h @ fc1_w + fc1_b)
        return z @ fc2_w + fc2_b

    def _L3_gnn_ref(ent_emb, rel_emb, neigh_w, src, dst, rel_id):
        import jax, jax.numpy as jnp
        import numpy as np
        N_ENT = 3125
        N_EDGE = 31250
        H_DIM = 128
        N_REL = 237
        n_nodes = ent_emb.shape[0]
        comp = ent_emb[src] + rel_emb[rel_id]
        score = jnp.sum(comp * ent_emb[dst], axis=-1)
        smax = jax.ops.segment_max(score, dst, num_segments=n_nodes)
        ex = jnp.exp(score - smax[dst])
        ssum = jax.ops.segment_sum(ex, dst, num_segments=n_nodes)
        norm = ex / ssum[dst]
        neigh = jax.ops.segment_sum(comp * norm[:, None], dst, num_segments=n_nodes)
        return jnp.tanh(neigh @ neigh_w)
    edge_index = jnp.stack([src, dst])
    h = jnp.maximum(_layernorm(x, axis=-1), 0.0)
    x = x + _L0_gnn_ref(h, L0_gnn_edge_emb, L0_gnn_q_w, L0_gnn_k_w, edge_index, edge_type_64, 0)
    h = jnp.maximum(_layernorm(x, axis=-1), 0.0)
    x = x + _L1_gnn_ref(h, edge_index, L1_gnn_Ws, L1_gnn_Wd, L1_gnn_att_s, L1_gnn_att_d, L1_gnn_b)
    h = jnp.maximum(_layernorm(x, axis=-1), 0.0)
    x = x + _L2_gnn_ref(h, src, dst, L2_gnn_W1, L2_gnn_b1, L2_gnn_W2, L2_gnn_b2, L2_gnn_fc1_w, L2_gnn_fc1_b, L2_gnn_fc2_w, L2_gnn_fc2_b)
    h = jnp.maximum(_layernorm(x, axis=-1), 0.0)
    x = x + _L3_gnn_ref(h, L3_gnn_rel_emb, L3_gnn_neigh_w, src, dst, edge_type_474)
    return x

_drawn_inputs = setup_inputs


def setup_inputs(seed=0):
    import zlib

    import numpy as np

    out = dict(_drawn_inputs(seed))
    spreads = {'L1_gnn_b': (0.0, 0.1),
     'L2_gnn_b1': (0.0, 0.597),
     'L2_gnn_b2': (0.0, 0.444),
     'L2_gnn_fc1_b': (0.0, 0.267),
     'L2_gnn_fc2_b': (0.0, 0.1)}
    factors = {'L1_gnn_Wd': 64.0, 'L1_gnn_att_s': 8.0, 'L1_gnn_att_d': 64.0}
    for name, (base, spread) in spreads.items():
        noise = np.random.default_rng([zlib.crc32(name.encode()), seed]).standard_normal(out[name].shape)
        drawn = base * np.exp(spread * noise) if base else spread * noise
        out[name] = jnp.asarray(drawn.astype(out[name].dtype))
    for name, factor in factors.items():
        out[name] = (out[name] * factor).astype(out[name].dtype)
    return out
```

```python
from contextlib import ExitStack

import concourse.bass as bass
from concourse import mybir

P = 128
D = 128
S = 8
H = 4
HALVES = S // H
CHUNKS = 17
RING = 4
BLANKS = 16

F32 = mybir.dt.float32
BF16 = mybir.dt.bfloat16
I32 = mybir.dt.int32
ALU = mybir.AluOpType
ACT = mybir.ActivationFunctionType
AX = mybir.AxisListType
RMAX = bass.bass_isa.ReduceOp.max
NEG = -1.0e30


class Shapes:
    def __init__(self, nodes, tiles):
        self.nodes = nodes
        self.blocks = -(-nodes // P)
        self.rows = self.blocks * P
        self.dummy = self.rows
        self.tiles = tiles
        self.steps = tiles // S
        self.chunks = CHUNKS
        self.stored = 16 * self.blocks
        self.bits = (self.rows - 1).bit_length()
        self.bodies = tiles * P // S + self.blocks


def stand(eng, turns, sem, value):
    eng.wait_ge(sem, value)
    eng.sem_inc(turns, 1)


def group_edges(nc, ctx, top, z, a, c, zero, consts):
    NB, TL, ST, CH, BITS = z.blocks, z.tiles, z.steps, z.chunks, z.bits
    CB = ST // CH
    CR = CB * S // (RING * H)
    ROUNDS = CH * CR
    CK = H * BITS
    V = nc.vector
    iota_row, iota_rb, iota_col, ident_b, before = consts
    NV = 11

    def sb(name, shape, dt=F32):
        return ctx.enter_context(nc.sbuf_tensor(name, shape, dt))

    def pb(name, shape, dt=F32):
        return ctx.enter_context(nc.psum_tensor(name, shape, dt))

    def sem(name):
        return top.sem(name)

    count = sb("count", [P, TL + 1, NB])
    key_i = sb("key_i", [P, TL], I32)
    part_i = sb("part_i", [P, TL], I32)
    key_f, lo_f, hi_f = sb("key_f", [P, TL]), sb("lo_f", [P, TL]), sb("hi_f", [P, TL])
    codes = sb("codes", [P, TL, BITS], BF16)
    pay = sb("pay", [P, 2, TL, 2], I32)
    found = sb("found", [P, TL, 2])
    ahead = sb("ahead", [P, TL])
    eighth_i = sb("eighth_i", [P, CB * S], I32)
    eighth = sb("eighth", [P, CB * S])
    position = sb("position", [P, 2, TL], I32)
    lo_hot = sb("lo_hot", [P, HALVES, H, P], BF16)
    hi_hot = sb("hi_hot", [P, HALVES, H, NB], BF16)
    loT = sb("loT", [P, HALVES, H, P])
    code_at = sb("code_at", [P, HALVES, H, BITS], BF16)
    codeT = sb("codeT", [CK, HALVES, P], BF16)
    diag = sb("diag", [CK, HALVES, H, P], BF16)
    block_mask = sb("block_mask", [CK, H])
    block_end = sb("block_end", [CK, H])
    matched_at = sb("matched_at", [P, HALVES, H, P], BF16)
    within = sb("within", [P, HALVES, H])
    hi_sel = sb("hi_sel", [P, HALVES, H, NB])
    picked = sb("picked", [P, HALVES, H, 2, NB])
    place = sb("place", [P, NB])
    order = sb("order", [P, NB])
    order_less = sb("order_less", [P, NB])
    order_row = sb("order_row", [P, z.rows])
    above_v = sb("above_v", [P, z.rows], BF16)
    above_a = sb("above_a", [P, z.rows], BF16)
    rank = sb("rank", [P, NB])
    rank_i = sb("rank_i", [P, NB], I32)
    rank_lo_i = sb("rank_lo_i", [P, NB], I32)
    rank_lo, rank_hi = sb("rank_lo", [P, NB]), sb("rank_hi", [P, NB])
    node_f = sb("node_f", [P, NB])
    pairs = sb("pairs", [P, NB, 2], I32)
    block_hot = sb("block_hot", [P, NB, NB])
    most = sb("most", [P, NB])
    nb_i = sb("nb_i", [P, NB], I32)
    nb_f, end_f, base_f = sb("nb_f", [P, NB]), sb("end_f", [P, NB]), sb("base_f", [P, NB])
    blank = sb("blank", [P, BLANKS * S, 2], I32)
    stage_at = sb("stage_at", [P, RING, H], I32)
    stage_pay = sb("stage_pay", [P, RING, H, 2], I32)
    counts_ps = [pb(f"counts_ps{h}", [P, H, NB]) for h in range(HALVES)]
    turned_ps = [pb(f"turned_ps{h}", [P, H + 1, P], BF16) for h in range(HALVES)]
    looked_ps = [pb(f"looked_ps{h}", [P, H, 2, NB]) for h in range(HALVES)]
    match_ps = [pb(f"match_ps{h}", [P, H, P]) for h in range(HALVES)]

    def pair(name):
        return [sem(f"{name}{h}") for h in range(HALVES)]

    key_in, pay_in, key_read = sem("key_in"), sem("pay_in"), sem("key_read")
    hots_ready, counts_ready, counts_kept = pair("hots_ready"), pair("counts_ready"), pair("counts_kept")
    dve, act_order = sem("dve_order"), sem("act_order")
    order_ready, order_out, order_in = sem("order_ready"), sem("order_out"), sem("order_in")
    ranked_by_act = sem("ranked_by_act")
    pairs_ready, pairs_out, perm_in = sem("pairs_ready"), sem("pairs_out"), sem("perm_in")
    deg_ready, most_ready, plan_ready, places_ready = (sem("deg_ready"), sem("most_ready"), sem("plan_ready"),
                                                       sem("places_ready"))
    lo_ready, turned, moved, diag_ready = pair("lo_ready"), pair("turned"), pair("moved"), pair("diag_ready")
    matched, behind, finished = pair("matched"), pair("behind"), pair("finished")
    position_ready = sem("position_ready")
    blank_out = [sem(f"blank_out{q}") for q in range(2)]
    staged, placed = [sem(f"staged{r}") for r in range(RING)], [sem(f"placed{r}") for r in range(RING)]
    turns = sem("turns")

    def blanks(total):
        return (total + (BLANKS + 1)) // BLANKS

    def natural(ap, cols=1):
        return ap.rearrange("(b p) c -> p b c", p=P) if cols > 1 else ap.rearrange("(b p) c -> p (b c)", p=P)

    with nc.Block() as block:

        @block.sync
        def _(sp):
            for q in range(2):
                if q:
                    sp.wait_ge(key_read, 1)
                sp.dma_start(key_i[:, :], a["key_cols"][q]).then_inc(key_in, 16)
                sp.dma_start(pay[:, q, :, :], a["payloads"][q]).then_inc(pay_in, 16)
            sp.wait_ge(pay_in, 32)
            for q in range(2):
                def put(r, i):
                    at = bass.ds(i * (RING * H) + r * H, H)
                    sp.dma_start(stage_at[:, r, :], position[:, q, at]).then_inc(staged[r], 16)
                    sp.dma_start(stage_pay[:, r, :, :], pay[:, q, at, :]).then_inc(staged[r], 16)

                for k in range(CH):
                    sp.wait_ge(position_ready, q * CH + k + 1)
                    first = k * CR
                    if q == 0 and k == 0:
                        for r in range(RING):
                            put(r, 0)
                        first = 1
                    with sp.Fori(first, (k + 1) * CR) as i:
                        for r in range(RING):
                            sp.wait_ge(placed[r], i * (16 * H) + 16 * H * q * ROUNDS)
                            put(r, i)

        @block.gpsimd
        def _(pool):
            for q in range(2):
                pool.wait_ge(pairs_ready, q + 1)
                for b in range(NB):
                    pool.indirect_dma_start(c.perm_dram[q][:, :], bass.IndirectOffsetOnAxis(ap=rank_i[:, b:b + 1], axis=0),
                                            pairs[:, b, :], None).then_inc(pairs_out, 16)
                pool.wait_ge(deg_ready, q + 1)
                nc.gpsimd.partition_all_reduce(most[:, :], c.degs[q][:, :], P, RMAX).then_inc(most_ready, 1)
                pool.wait_ge(plan_ready, q + 1)
                total = pool.value_load(c.plans[q][0:1, 2 * NB:2 * NB + 1], min_val=NB, max_val=z.bodies)
                stand(pool, turns, blank_out[q], blanks(total) * 16)
                with pool.Fori(0, ROUNDS) as i:
                    for r in range(RING):
                        stand(pool, turns, staged[r], i * 32 + 32 * (q * ROUNDS + 1))
                        for j in range(H):
                            pool.indirect_dma_start(
                                c.ells[q][:, :], bass.IndirectOffsetOnAxis(ap=stage_at[:, r, j:j + 1], axis=0),
                                stage_pay[:, r, j, :], None).then_inc(placed[r], 16)
            for r in range(RING):
                pool.wait_ge(placed[r], 16 * H * 2 * ROUNDS)

        @block.tensor
        def _(pe):
            for q in range(2):
                with pe.Fori(0, ST) as i:
                    for h in range(HALVES):
                        pe.wait_ge(hots_ready[h], i + (q * ST + 1))
                        pe.wait_ge(counts_kept[h], i + (q * ST + 1))
                        for j in range(H):
                            mm = pe.matmul(counts_ps[h][:, j, :], lo_hot[:, h, j, :], hi_hot[:, h, j, :],
                                           start=True, stop=True)
                        mm.then_inc(counts_ready[h], 1)
                pe.wait_ge(places_ready, q + 1)

                def turn(h, i, n):
                    pe.wait_ge(lo_ready[h], n + 1)
                    for j in range(H):
                        pe.transpose(turned_ps[h][:, j, :], lo_hot[:, h, j, :], ident_b[:, :])
                    pe.transpose(turned_ps[h][0:CK, H, :], code_at[:, h, :, :].rearrange("p j b -> p (j b)"),
                                 ident_b[:, :]).then_inc(turned[h], 1)

                def look(h, i, n):
                    pe.wait_ge(moved[h], n + 1)
                    pe.wait_ge(finished[h], n + 1)
                    for j in range(H):
                        pe.matmul(looked_ps[h][:, j, 0, :], loT[:, h, j, :],
                                  count[:, bass.ds(i * S + (h * H + j), 1), :].rearrange("p a n -> p (a n)"),
                                  start=True, stop=True)
                        pe.matmul(looked_ps[h][:, j, 1, :], loT[:, h, j, :], place[:, :], start=True, stop=True)
                    pe.wait_ge(diag_ready[h], n + 1)
                    pe.matmul(match_ps[h][:, :, :].rearrange("p j e -> p (j e)"), codeT[:, h, :],
                              diag[:, h, :, :].rearrange("p j e -> p (j e)"), start=True, stop=False)
                    pe.matmul(match_ps[h][:, :, :].rearrange("p j e -> p (j e)"), ident_b[:, :],
                              before[:, :, :].rearrange("p j e -> p (j e)"),
                              start=False, stop=True).then_inc(matched[h], 1)

                with pe.Fori(0, CH) as k:
                    at = k * CB
                    turn(0, at, at + q * ST)
                    turn(1, at, at + q * ST)
                    look(0, at, at + q * ST)
                    with pe.Fori(1, CB) as s:
                        i = at + s
                        turn(0, i, i + q * ST)
                        look(1, i + (-1), i + (q * ST - 1))
                        turn(1, i, i + q * ST)
                        look(0, i, i + q * ST)
                    look(1, at + (CB - 1), at + (q * ST + CB - 1))

        @block.scalar
        def _(act):
            for h in range(HALVES):
                act.sem_inc(counts_kept[h], 1)
            for q in range(2):
                with act.Fori(0, ST) as i:
                    for h in range(HALVES):
                        act.wait_ge(counts_ready[h], i + (q * ST + 1))
                        nc.scalar.copy(count[:, bass.ds(i * S + (h * H + 1), H), :],
                                       counts_ps[h][:, :, :]).then_inc(counts_kept[h], 1)
                act.wait_ge(order_ready, q + 1)
                act.dma_start(natural(c.order_dram), order[:, :], allow_slow_non_contiguous=True).then_inc(order_out, 16)
                act.dma_start(natural(c.degree_dram[q]), c.natural_deg[:, q, :],
                              allow_slow_non_contiguous=True).then_inc(order_out, 16)
                act.wait_ge(order_out, 32 * (q + 1))
                act.dma_start(order_row[:, :], c.order_dram.rearrange("n a -> a n")
                              .to_broadcast([P, z.rows])).then_inc(order_in, 16)
                act.wait_ge(order_in, 16 * (q + 1))
                for b in range(NV, NB):
                    last = nc.scalar.activation(above_a[:, :], order_row[:, :], ACT.Sign, bias=order_less[:, b:b + 1],
                                                accum_out=rank[:, b:b + 1])
                    last.then_inc(act_order, 1)
                    act.wait_ge(act_order, q * (NB - NV) + b - NV + 1)
                act.sem_inc(ranked_by_act, 1)
                act.wait_ge(pairs_out, 16 * NB * (q + 1))
                act.dma_start(c.perms[q][:, :, :], natural(c.perm_dram[q], 2)).then_inc(perm_in, 16)
                act.wait_ge(plan_ready, q + 1)
                total = act.value_load(c.plans[q][0:1, 2 * NB:2 * NB + 1], min_val=NB, max_val=z.bodies)
                with act.Fori(0, blanks(total)) as i:
                    act.dma_start(c.ells[q][bass.ds(i * (BLANKS * S * P), BLANKS * S * P), :]
                                  .rearrange("(p s) c -> p (s c)", p=P),
                                  blank[:, :, :].rearrange("p s c -> p (s c)")).then_inc(blank_out[q], 16)

                def move(h, n):
                    act.wait_ge(turned[h], n + 1)
                    nc.scalar.copy(codeT[:, h, :], turned_ps[h][0:CK, H, :])
                    nc.scalar.copy(loT[:, h, :, :], turned_ps[h][:, 0:H, :]).then_inc(moved[h], 1)

                def tell(h, n):
                    act.wait_ge(matched[h], n + 2)
                    for j in range(H):
                        last = nc.scalar.activation(matched_at[:, h, j, :], match_ps[h][:, j, :], ACT.Relu,
                                                    accum_out=within[:, h, j:j + 1])
                    last.then_inc(behind[h], 1)

                with act.Fori(0, CH) as k:
                    at = k * CB + q * ST
                    for h in range(HALVES):
                        move(h, at)
                    with act.Fori(1, CB) as s:
                        n = at + s
                        for h in range(HALVES):
                            tell(h, n + (-1))
                            move(h, n)
                    for h in range(HALVES):
                        tell(h, at + (CB - 1))

        @block.vector
        def _(v):
            done = [0]

            def step(ins):
                done[0] += 1
                ins.then_inc(dve, 1)
                v.wait_ge(dve, done[0])

            V.memset(blank[:, :, 0:1], z.dummy)
            V.memset(blank[:, :, 1:2], 0)
            V.tensor_scalar(block_end[:, :], iota_row[0:CK, 0:H], float(BITS), None, ALU.mult)
            v.drain()
            V.tensor_scalar(block_mask[:, :], block_end[:, :], iota_col[0:CK, 0:1], None, ALU.is_le)
            V.tensor_scalar(block_end[:, :], block_end[:, :], float(BITS), None, ALU.add)
            v.drain()
            V.scalar_tensor_tensor(out=block_mask[:, :], in0=block_end[:, :], scalar=iota_col[0:CK, 0:1],
                                   in1=block_mask[:, :], op0=ALU.is_gt, op1=ALU.mult)
            V.tensor_scalar(node_f[:, :], iota_row[:, 0:NB], float(P), iota_col[:, 0:1], ALU.mult, ALU.add)
            for h in range(HALVES):
                v.sem_inc(finished[h], 1)
                v.sem_inc(matched[h], 1)

            for q in range(2):
                v.wait_ge(key_in, 16 * (q + 1))
                V.tensor_copy(key_f[:, :], key_i[:, :])
                V.tensor_scalar(part_i[:, :], key_i[:, :], P - 1, None, ALU.bitwise_and)
                v.drain()
                V.tensor_copy(lo_f[:, :], part_i[:, :])
                v.drain()
                V.tensor_tensor(hi_f[:, :], key_f[:, :], lo_f[:, :], ALU.subtract)
                for k in range(BITS):
                    v.drain()
                    V.tensor_scalar(part_i[:, :], key_i[:, :], k, 1, ALU.arith_shift_right, ALU.bitwise_and)
                    v.drain()
                    V.tensor_scalar(codes[:, :, k], part_i[:, :], 2.0, -1.0, ALU.mult, ALU.add)
                step(V.tensor_scalar(hi_f[:, :], hi_f[:, :], 1.0 / P, None, ALU.mult))
                v.sem_inc(key_read, 1)
                V.memset(count[:, 0, :], 0.0)

                def low(h, i):
                    return V.tensor_tensor(
                        lo_hot[:, h, :, :], spread(iota_rb[:, :], [P, H, P], 1),
                        spread(lo_f[:, bass.ds(i * S + h * H, H)], [P, H, P], 2), ALU.is_equal)

                def hots(h, i):
                    low(h, i)
                    V.tensor_tensor(
                        hi_hot[:, h, :, :], spread(iota_row[:, 0:NB], [P, H, NB], 1),
                        spread(hi_f[:, bass.ds(i * S + h * H, H)], [P, H, NB], 2),
                        ALU.is_equal).then_inc(hots_ready[h], 1)

                for h in range(HALVES):
                    hots(h, 0)
                with v.Fori(1, ST) as i:
                    for h in range(HALVES):
                        v.wait_ge(counts_ready[h], i + q * ST)
                        hots(h, i)
                for h in range(HALVES):
                    v.wait_ge(counts_kept[h], 1 + (q + 1) * ST)
                for b in range(NB):
                    V.tensor_tensor_scan(count[:, :, b], count[:, :, b], zero[:, 0:1].to_broadcast([P, TL + 1]), 0.0,
                                         ALU.add, ALU.add)
                v.drain()

                deg = c.natural_deg[:, q, :]
                step(V.tensor_copy(deg, count[:, TL, :]))
                step(V.tensor_scalar(order[:, :], deg, 4095.0, 4096.0, ALU.min, ALU.mult))
                step(V.tensor_tensor(order[:, :], order[:, :], node_f[:, :], ALU.subtract))
                V.tensor_scalar(order_less[:, :], order[:, :], -1.0, None, ALU.mult).then_inc(order_ready, 1)
                V.tensor_copy(pairs[:, :, 0], node_f[:, :])
                V.tensor_copy(pairs[:, :, 1], deg)
                v.wait_ge(order_in, 16 * (q + 1))
                for b in range(NV):
                    step(V.tensor_scalar(above_v[:, :], order_row[:, :], order[:, b:b + 1], None, ALU.is_gt, ALU.add,
                                         accum_out=rank[:, b:b + 1]))
                v.wait_ge(ranked_by_act, q + 1)
                step(V.tensor_scalar(rank[:, NV:NB], rank[:, NV:NB], 0.5, 0.5 * (z.rows - 1), ALU.mult, ALU.add))
                step(V.tensor_copy(rank_i[:, :], rank[:, :]))
                v.sem_inc(pairs_ready, 1)
                step(V.tensor_scalar(rank_lo_i[:, :], rank_i[:, :], P - 1, None, ALU.bitwise_and))
                step(V.tensor_copy(rank_lo[:, :], rank_lo_i[:, :]))
                step(V.tensor_tensor(rank_hi[:, :], rank[:, :], rank_lo[:, :], ALU.subtract))
                step(V.tensor_scalar(rank_hi[:, :], rank_hi[:, :], 1.0 / P, None, ALU.mult))
                step(V.tensor_tensor(block_hot[:, :, :], spread(iota_row[:, 0:NB], [P, NB, NB], 1),
                                     spread(rank_hi[:, :], [P, NB, NB], 2), ALU.is_equal))

                v.wait_ge(perm_in, 16 * (q + 1))
                V.tensor_copy(c.degs[q][:, :], c.perms[q][:, :, 1]).then_inc(deg_ready, 1)
                v.wait_ge(most_ready, q + 1)
                step(V.tensor_scalar(nb_i[:, :], most[:, :], float(S - 1), None, ALU.add))
                step(V.tensor_scalar(nb_i[:, :], nb_i[:, :], 3, None, ALU.arith_shift_right))
                step(V.tensor_copy(nb_f[:, :], nb_i[:, :]))
                step(V.tensor_scalar(nb_f[:, :], nb_f[:, :], 1.0, None, ALU.max))
                step(V.tensor_tensor_scan(end_f[:, :], nb_f[:, :], zero[:, 0:1].to_broadcast([P, NB]), 0.0,
                                          ALU.add, ALU.add))
                step(V.tensor_tensor(base_f[:, :], end_f[:, :], nb_f[:, :], ALU.subtract))
                V.tensor_copy(c.plans[q][:, 0:NB], nb_f[:, :])
                V.tensor_copy(c.plans[q][:, NB:2 * NB], base_f[:, :])
                step(V.tensor_copy(c.plans[q][:, 2 * NB:2 * NB + 1], end_f[:, NB - 1:NB]))
                v.sem_inc(plan_ready, 1)
                step(V.tensor_tensor(block_hot[:, :, :], block_hot[:, :, :], spread(base_f[:, :], [P, NB, NB], 1),
                                     ALU.mult))
                step(V.tensor_reduce(place[:, :], block_hot[:, :, :], AX.X, ALU.add))
                step(V.scalar_tensor_tensor(out=place[:, :], in0=place[:, :], scalar=float(P), in1=rank_lo[:, :],
                                            op0=ALU.mult, op1=ALU.add))
                step(V.tensor_scalar(place[:, :], place[:, :], float(S), None, ALU.mult))
                v.sem_inc(places_ready, 1)

                def lows(h, i):
                    V.tensor_copy(code_at[:, h, :, :], codes[:, bass.ds(i * S + h * H, H), :])
                    low(h, i).then_inc(lo_ready[h], 1)

                def diagonal(h, n):
                    v.wait_ge(moved[h], n + 1)
                    v.wait_ge(matched[h], n + 1)
                    V.tensor_tensor(diag[:, h, :, :], spread(codeT[:, h, :], [CK, H, P], 1),
                                    spread(block_mask[:, :], [CK, H, P], 2), ALU.mult).then_inc(diag_ready[h], 1)

                def finish(h, i, n):
                    at = bass.ds(i * S + h * H, H)
                    V.tensor_tensor(hi_sel[:, h, :, :], spread(iota_row[:, 0:NB], [P, H, NB], 1),
                                    spread(hi_f[:, at], [P, H, NB], 2), ALU.is_equal)
                    v.drain()
                    v.wait_ge(behind[h], n + 1)
                    V.tensor_tensor(picked[:, h, :, :, :], looked_ps[h][:, :, :, :],
                                    spread(hi_sel[:, h, :, :], [P, H, 2, NB], 2), ALU.mult)
                    V.tensor_copy(ahead[:, at], within[:, h, :])
                    v.drain()
                    v.sem_inc(finished[h], 1)
                    V.tensor_reduce(found[:, at, :], picked[:, h, :, :, :], AX.X, ALU.add)

                with v.Fori(0, CH) as k:
                    at = k * CB
                    lows(0, at)
                    lows(1, at)
                    diagonal(0, at + q * ST)
                    with v.Fori(1, CB) as s:
                        i = at + s
                        lows(0, i)
                        diagonal(1, i + (q * ST - 1))
                        finish(0, i + (-1), i + (q * ST - 1))
                        lows(1, i)
                        diagonal(0, i + q * ST)
                        finish(1, i + (-1), i + (q * ST - 1))
                    diagonal(1, at + (q * ST + CB - 1))
                    for h in range(HALVES):
                        finish(h, at + (CB - 1), at + (q * ST + CB - 1))
                    v.drain()
                    part = bass.ds(k * (CB * S), CB * S)
                    V.tensor_tensor(ahead[:, part], ahead[:, part], found[:, part, 0], ALU.add)
                    v.drain()
                    V.tensor_copy(eighth_i[:, :], ahead[:, part])
                    v.drain()
                    V.tensor_scalar(eighth_i[:, :], eighth_i[:, :], 3, None, ALU.arith_shift_right)
                    v.drain()
                    V.tensor_copy(eighth[:, :], eighth_i[:, :])
                    v.drain()
                    V.scalar_tensor_tensor(out=ahead[:, part], in0=eighth[:, :], scalar=float(S * P - S),
                                           in1=ahead[:, part], op0=ALU.mult, op1=ALU.add)
                    v.drain()
                    V.tensor_tensor(position[:, q, part], ahead[:, part], found[:, part, 1], ALU.add)
                    v.drain()
                    v.sem_inc(position_ready, 1)


class Semaphores:

    def __init__(self, nc):
        self.nc, self.held = nc, []

    def __enter__(self):
        return self

    def sem(self, name):
        self.held.append(self.nc.alloc_semaphore(name=name))
        return self.held[-1]

    def __exit__(self, *failure):
        if failure[0] is None:
            self.nc.all_engine_barrier()
            self.nc.clear_and_free_semaphores(self.held)
            self.nc.all_engine_barrier()


class Projection:

    def __init__(self, nc, ctx, top, z, name, chunks, width):
        self.nc, self.z, self.chunks, self.width = nc, z, chunks, width
        self.group = 5
        self.groups = z.blocks // self.group
        assert self.groups * self.group == z.blocks
        per_bank = 512 // width
        room = -(-self.group // per_bank) * per_bank
        turned = -(-self.group * chunks // 4) * 4
        self.turned_ps = ctx.enter_context(nc.psum_tensor(f"{name}_turned_ps", [P, turned, P], F32))
        self.product_ps = ctx.enter_context(nc.psum_tensor(f"{name}_product_ps", [P, room, width], F32))
        self.turned_sb = ctx.enter_context(nc.sbuf_tensor(f"{name}_turned_sb", [P, self.group * chunks, P], F32))
        self.source_ready = top.sem(f"{name}_source_ready")
        self.turned = top.sem(f"{name}_turned")
        self.moved = top.sem(f"{name}_moved")
        self.projected = top.sem(f"{name}_projected")
        self.taken = top.sem(f"{name}_taken")

    def open(self, v):
        v.sem_inc(self.taken, 1)

    def tensor(self, pe, use, source, weights, ident):
        pe.wait_ge(self.source_ready, use + 1)
        for g in range(self.groups):
            n = use * self.groups + (g + 1)
            for k in range(self.group):
                for c in range(self.chunks):
                    mm = pe.transpose(self.turned_ps[:, k * self.chunks + c, :],
                                      source(g * self.group + k, c), ident)
            mm.then_inc(self.turned, 1)
            pe.wait_ge(self.moved, n)
            pe.wait_ge(self.taken, n)
            for k in range(self.group):
                for c in range(self.chunks):
                    mm = pe.matmul(self.product_ps[:, k, :], self.turned_sb[:, k * self.chunks + c, :],
                                   weights(c), start=(c == 0), stop=(c == self.chunks - 1))
            mm.then_inc(self.projected, 1)

    def scalar(self, act, use):
        with act.Fori(0, self.groups) as g:
            act.wait_ge(self.turned, use * self.groups + g + 1)
            self.nc.scalar.copy(self.turned_sb[:, :, :],
                                self.turned_ps[:, 0:self.group * self.chunks, :]).then_inc(self.moved, 1)

    def vector(self, v, use, take):
        with v.Fori(0, self.groups) as g:
            v.wait_ge(self.projected, use * self.groups + g + 1)
            take(g * self.group, self.product_ps[:, 0:self.group, :]).then_inc(self.taken, 1)
        v.drain()


def spread(ap, shape, axis):
    return ap.unsqueeze(axis).to_broadcast(shape)


def normalize(nc, top, z, name, x, h, work, col):
    NB = z.blocks
    order = top.sem(f"{name}_order")
    spread_ready = top.sem(f"{name}_spread_ready")
    root_ready = top.sem(f"{name}_root_ready")
    with nc.Block() as block:
        @block.vector
        def _(v):
            wide = [P, NB, D]
            nc.vector.tensor_reduce(col[:, 0, :], x[:, :, :], AX.X, ALU.add)
            v.drain()
            nc.vector.tensor_scalar(col[:, 0, :], col[:, 0, :], 1.0 / D, None, ALU.mult)
            v.drain()
            nc.vector.tensor_tensor(h[:, :, :], x[:, :, :], spread(col[:, 0, :], wide, 2), ALU.subtract)
            v.drain()
            nc.vector.tensor_tensor(work[:, :, :], h[:, :, :], h[:, :, :], ALU.mult)
            v.drain()
            nc.vector.tensor_reduce(col[:, 1, :], work[:, :, :], AX.X, ALU.add)
            v.drain()
            nc.vector.tensor_scalar(col[:, 1, :], col[:, 1, :], 1.0 / D, 1e-5, ALU.mult,
                                    ALU.add).then_inc(spread_ready, 1)
            v.wait_ge(root_ready, 1)
            nc.vector.reciprocal(col[:, 3, :], col[:, 2, :])
            v.drain()
            nc.vector.tensor_tensor(h[:, :, :], h[:, :, :], spread(col[:, 3, :], wide, 2), ALU.mult)
            v.drain()
            nc.vector.tensor_scalar(h[:, :, :], h[:, :, :], 0.0, None, ALU.max).then_inc(order, 1)
            v.wait_ge(order, 1)

        @block.scalar
        def _(act):
            act.wait_ge(spread_ready, 1)
            nc.scalar.activation(col[:, 2, :], col[:, 1, :], ACT.Sqrt).then_inc(root_ready, 1)


def scatter_rows(pool, z, perm, table, rows, sem):
    for b in range(z.blocks):
        pool.indirect_dma_start(table[:, :], bass.IndirectOffsetOnAxis(ap=perm[:, b, 0:1], axis=0),
                                rows[:, b, :], None).then_inc(sem, 16)


def gather_rows(pool, z, perm, table, rows, sem):
    for b in range(z.blocks):
        pool.indirect_dma_start(rows[:, b, :], None, table[:, :],
                                bass.IndirectOffsetOnAxis(ap=perm[:, b, 0:1], axis=0)).then_inc(sem, 16)


class Stream:

    def __init__(self, nc, ctx, top, z, name, ell, plan, width, sources=1):
        self.nc, self.z, self.ell, self.plan = nc, z, ell, plan
        self.per_half = 16 * H * sources
        self.index = ctx.enter_context(nc.sbuf_tensor(f"{name}_index", [P, HALVES, H, 2], I32))
        self.land = ctx.enter_context(nc.sbuf_tensor(f"{name}_land", [P, S, width], F32))

        def sem(what):
            return top.sem(f"{name}_{what}")

        self.index_in = [sem(f"index_in{h}") for h in range(HALVES)]
        self.landed = [sem(f"landed{h}") for h in range(HALVES)]
        self.land_free = [sem(f"land_free{h}") for h in range(HALVES)]
        self.table_in = sem("table_in")
        self.turns = sem("turns")

    def total(self, eng):
        NB = self.z.blocks
        return eng.value_load(self.plan[0:1, 2 * NB:2 * NB + 1], min_val=NB, max_val=self.z.bodies)

    def block(self, eng, b):
        NB = self.z.blocks
        many = eng.value_load(self.plan[0:1, bass.ds(b, 1)], min_val=1, max_val=self.z.bodies)
        first = eng.value_load(self.plan[0:1, bass.ds(b + NB, 1)], min_val=0, max_val=self.z.bodies)
        return many, first

    def part(self, body, h):
        return self.ell[bass.ds(body * (S * P), S * P), :].rearrange("(p s) c -> p s c", p=P)[:, h * H:(h + 1) * H, :]

    def load(self, sp, n, body, h, first=False):
        if not first:
            sp.wait_ge(self.landed[h], n * self.per_half)
        sp.dma_start(self.index[:, h, :, :], self.part(body, h)).then_inc(self.index_in[h], 16)

    def load_all(self, sp, hop, bodies):
        for h in range(HALVES):
            self.load(sp, 0, 0, h, first=True)
        with sp.Fori(1, bodies) as body:
            for h in range(HALVES):
                self.load(sp, hop * bodies + body, body, h)

    def gather(self, pool, n, h, sources):
        stand(pool, self.turns, self.index_in[h], n * 16 + 16)
        stand(pool, self.turns, self.land_free[h], n + 1)
        for j in range(H):
            for table, c, land in sources:
                pool.indirect_dma_start(
                    land[:, h * H + j, :], None, table[:, :],
                    bass.IndirectOffsetOnAxis(ap=self.index[:, h, j, c:c + 1], axis=0)).then_inc(self.landed[h], 16)


class Softmax:

    def __init__(self, nc, ctx, top, name, heads):
        self.nc, self.heads = nc, heads

        def sb(what, shape):
            return ctx.enter_context(nc.sbuf_tensor(f"{name}_{what}", shape, F32))

        self.score = sb("score", [P, S, heads])
        self.absent = sb("absent", [P, S])
        self.left = sb("left_over", [P, 1])
        self.top_now = sb("top_now", [P, heads])
        self.top_body = sb("top_body", [P, heads])
        self.top_new = sb("top_new", [P, heads])
        self.drop = sb("drop", [P, heads])
        self.prob = sb("prob", [P, S, heads])
        self.keep = sb("keep", [P, heads])
        self.part = sb("prob_sum", [P, heads])
        self.denom = sb("denom", [P, heads])
        self.score_ready = top.sem(f"{name}_score_ready")
        self.prob_ready = top.sem(f"{name}_prob_ready")

    def begin(self, degree):
        self.nc.vector.memset(self.top_now[:, :], NEG)
        self.nc.vector.memset(self.denom[:, :], 0.0)
        self.nc.vector.tensor_copy(self.left[:, :], degree)

    def mark(self, iota_row):
        self.nc.vector.tensor_scalar(self.absent[:, :], iota_row[:, 0:S], self.left[:, 0:1], NEG, ALU.is_ge, ALU.mult)

    def scores(self, v):
        V, n = self.nc.vector, self.heads
        V.tensor_scalar(self.left[:, :], self.left[:, :], float(-S), None, ALU.add)
        V.tensor_tensor(self.score[:, :, :], self.score[:, :, :], spread(self.absent[:, :], [P, S, n], 2), ALU.add)
        v.drain()
        V.tensor_reduce(self.top_body[:, :], self.score[:, :, :].rearrange("p s h -> p h s"), AX.X, ALU.max)
        v.drain()
        V.tensor_tensor(self.top_new[:, :], self.top_now[:, :], self.top_body[:, :], ALU.max)
        v.drain()
        V.tensor_tensor(self.drop[:, :], self.top_now[:, :], self.top_new[:, :], ALU.subtract)
        V.tensor_tensor(self.score[:, :, :], self.score[:, :, :], spread(self.top_new[:, :], [P, S, n], 1),
                        ALU.subtract).then_inc(self.score_ready, 1)

    def exponentials(self, act, n):
        act.wait_ge(self.score_ready, n + 1)
        self.nc.scalar.activation(self.keep[:, :], self.drop[:, :], ACT.Exp)
        self.nc.scalar.activation(self.prob[:, :, :], self.score[:, :, :], ACT.Exp).then_inc(self.prob_ready, 1)

    def weigh(self, v, n, values, weighed, total, part, width, meanwhile=None):
        V, h = self.nc.vector, self.heads
        c = width // h
        v.wait_ge(self.prob_ready, n + 1)
        V.tensor_copy(self.top_now[:, :], self.top_new[:, :])
        ins = V.tensor_tensor(weighed[:, :, :].rearrange("p s (h c) -> p s h c", h=h),
                              values.rearrange("p s (h c) -> p s h c", h=h),
                              spread(self.prob[:, :, :], [P, S, h, c], 3), ALU.mult)
        if meanwhile is not None:
            meanwhile()
        V.tensor_reduce(self.part[:, :], self.prob[:, :, :].rearrange("p s h -> p h s"), AX.X, ALU.add)
        V.tensor_tensor(self.denom[:, :], self.denom[:, :], self.keep[:, :], ALU.mult)
        V.tensor_tensor(total[:, :].rearrange("p (h c) -> p h c", h=h), total[:, :].rearrange("p (h c) -> p h c", h=h),
                        spread(self.keep[:, :], [P, h, c], 2), ALU.mult)
        v.drain()
        V.tensor_reduce(part[:, :], weighed[:, :, :].rearrange("p s f -> p f s"), AX.X, ALU.add)
        V.tensor_tensor(self.denom[:, :], self.denom[:, :], self.part[:, :], ALU.add)
        v.drain()
        V.tensor_tensor(total[:, :], total[:, :], part[:, :], ALU.add)
        return ins


def attention_over_relations(nc, top, z, c, a, x, h, res, work):
    NB, HOPS, KINDS = z.blocks, 3, 64
    with ExitStack() as ctx:
        def sb(name, shape, dt=F32):
            return ctx.enter_context(nc.sbuf_tensor(name, shape, dt))

        def sem(name):
            return top.sem(name)

        q_w, k_w = sb("q_w", [P, D]), sb("k_w", [P, D])
        relation = sb("relation", [P, D])
        rest = sb("rest", [P, D])
        parts = sb("relation_parts", [P, 3, 2, D], BF16)
        left, left_now = sb("left", [P, NB, D]), sb("left_now", [P, D])
        kind = sb("kind", [P, HALVES, H, 2], I32)
        hot = sb("hot", [P, HALVES, H, KINDS], BF16)
        hotT = sb("hotT", [P, HALVES, H // 2, P], BF16)
        message = sb("message", [P, S, D])
        kept = sb("kept", [P, 2, S, D])
        messageT = sb("messageT", [P, HALVES, H, P])
        right = sb("right", [P, S, D])
        product = sb("product", [P, S, D])
        total, part = sb("total", [P, D]), sb("part", [P, D])
        scale = sb("scale", [P, 1])
        share = sb("share", [P, NB])
        col = sb("norm_col", [P, 4, NB])
        stream = Stream(nc, ctx, top, z, "l0", c.ells[0], c.plans[0], D)
        soft = Softmax(nc, ctx, top, "l0", 1)
        kind_in = [sem(f"kind_in{k}") for k in range(HALVES)]
        kind_free = [sem(f"kind_free{k}") for k in range(HALVES)]
        hot_ready = [sem(f"hot_ready{k}") for k in range(HALVES)]
        hotT_ready = [sem(f"hotT_ready_rel{k}") for k in range(HALVES)]
        hotT_moved = [sem(f"hotT_moved{k}") for k in range(HALVES)]
        rel_ready = [sem(f"rel_ready{k}") for k in range(HALVES)]
        message_ready = [sem(f"message_ready{k}") for k in range(HALVES)]
        messageT_ready = [sem(f"messageT_ready{k}") for k in range(HALVES)]
        messageT_moved = [sem(f"messageT_moved{k}") for k in range(HALVES)]
        right_ready = [sem(f"right_ready{k}") for k in range(HALVES)]
        right_out = [sem(f"right_out{k}") for k in range(HALVES)]
        right_used = [sem(f"right_used{k}") for k in range(HALVES)]
        kept_ready = [sem(f"kept_ready{k}") for k in range(HALVES)]
        weights_in = sem("l0_weights_in")
        sums_ready = sem("l0_sums_ready")
        norms_ready = sem("l0_norms_ready")
        proj = Projection(nc, ctx, top, z, "left", 1, D)
        hotT_ps = ctx.enter_context(nc.psum_tensor("hotT_ps", [P, HALVES, 2 * H, P], BF16))
        messageT_ps = proj.turned_ps
        right_ps = proj.product_ps
        rel_ps = ctx.enter_context(nc.psum_tensor("rel_ps", [P, S, P], F32))

        with nc.Block() as block:

            @block.sync
            def _(sp):
                sp.dma_start(q_w[:, :], a["q_w"]).then_inc(weights_in, 16)
                sp.dma_start(k_w[:, :], a["k_w"]).then_inc(weights_in, 16)
                for k in range(2):
                    sp.dma_start(relation[k * KINDS:(k + 1) * KINDS, :], a["edge_emb"]).then_inc(weights_in, 16)
                for k in range(HALVES):
                    sp.sem_inc(kind_free[k], 1)
                all_bodies = stream.total(sp)
                with sp.Fori(0, HOPS) as hop:
                    sp.wait_ge(proj.source_ready, hop + 1)

                    def kinds(body):
                        for k in range(HALVES):
                            sp.wait_ge(kind_free[k], hop * (all_bodies + 2) + body + 1)
                            sp.dma_start(kind[:, k, :, :], stream.part(body, k)).then_inc(kind_in[k], 16)

                    kinds(0)
                    for k in range(HALVES):
                        stream.load(sp, 0, 0, k, first=True)
                    with sp.Fori(1, all_bodies + 1) as body:
                        kinds(body)
                        for k in range(HALVES):
                            stream.load(sp, hop * (all_bodies + 1) + body, body, k)
                    kinds(all_bodies + 1)

            @block.gpsimd
            def _(pool):
                all_bodies = stream.total(pool)
                with pool.Fori(0, HOPS) as hop:
                    pool.wait_ge(proj.source_ready, hop + 1)
                    pool.sem_inc(stream.turns, 1)
                    scatter_rows(pool, z, c.perms[0], c.table, res, stream.table_in)
                    stand(pool, stream.turns, stream.table_in, hop * z.stored + z.stored)
                    with pool.Fori(0, all_bodies + 1) as body:
                        for k in range(HALVES):
                            stream.gather(pool, hop * (all_bodies + 1) + body, k, [(c.table, 0, stream.land)])

            @block.tensor
            def _(pe):
                all_bodies = stream.total(pe)
                pe.wait_ge(weights_in, 64)

                def turn_kinds(m):
                    for k in range(HALVES):
                        pe.wait_ge(hot_ready[k], m + 1)
                        for j in range(H // 2):
                            mm = pe.transpose(hotT_ps[:, k, j, :],
                                              hot[:, k, 2 * j:2 * j + 2, :].rearrange("p s n -> p (s n)"),
                                              c.ident_b[:, :])
                        mm.then_inc(hotT_ready[k], 1)

                def relations(m, k):
                    pe.wait_ge(hotT_moved[k], m + 2)
                    for j in range(H // 2):
                        pair = slice(k * H + 2 * j, k * H + 2 * j + 2)
                        for t in range(3):
                            mm = pe.matmul(rel_ps[:, pair, :].rearrange("p s d -> p (s d)"), hotT[:, k, j, :],
                                           parts[:, t, :, :].rearrange("p s d -> p (s d)"), start=(t == 0), stop=(t == 2))
                    mm.then_inc(rel_ready[k], 1)

                def rights(n, k):
                    pe.wait_ge(message_ready[k], n + 1)
                    for j in range(H):
                        mm = pe.transpose(messageT_ps[:, k * H + j, :], message[:, k * H + j, :], c.ident[:, :])
                    mm.then_inc(messageT_ready[k], 1)
                    pe.wait_ge(messageT_moved[k], n + 1)
                    pe.wait_ge(right_out[k], n + 1)
                    for j in range(H):
                        mm = pe.matmul(right_ps[:, k * H + j, :], messageT[:, k, j, :], k_w[:, :],
                                       start=True, stop=True)
                    mm.then_inc(right_ready[k], 1)

                with pe.Fori(0, HOPS) as hop:
                    n, m = pe.snap(hop * (all_bodies + 1)), pe.snap(hop * (all_bodies + 2))
                    proj.tensor(pe, hop, lambda b, _: res[:, b, :], lambda _: q_w[:, :], c.ident[:, :])
                    turn_kinds(m)
                    for k in range(HALVES):
                        relations(m, k)
                    turn_kinds(m + 1)
                    for k in range(HALVES):
                        rights(n, k)
                        relations(m + 1, k)
                    with pe.Fori(0, all_bodies) as i:
                        turn_kinds(m + i + 2)
                        for k in range(HALVES):
                            rights(n + i + 1, k)
                            relations(m + i + 2, k)

            @block.scalar
            def _(act):
                all_bodies = stream.total(act)
                for k in range(HALVES):
                    act.sem_inc(kept_ready[k], 1)
                    act.sem_inc(right_out[k], 1)
                    act.sem_inc(hotT_moved[k], 1)

                def move_kinds(m):
                    for k in range(HALVES):
                        act.wait_ge(hotT_ready[k], m + 1)
                        nc.scalar.copy(hotT[:, k, :, :], hotT_ps[:, k, 0:H // 2, :]).then_inc(hotT_moved[k], 1)

                def move_messages(n, k):
                    half = slice(k * H, (k + 1) * H)
                    act.wait_ge(messageT_ready[k], n + 1)
                    nc.scalar.copy(messageT[:, k, :, :], messageT_ps[:, half, :]).then_inc(messageT_moved[k], 1)
                    nc.scalar.copy(kept[:, bass.ds(n % 2, 1), half, :].rearrange("p a s d -> p (a s) d"),
                                   message[:, half, :]).then_inc(kept_ready[k], 1)

                def tanh(n, k):
                    half = slice(k * H, (k + 1) * H)
                    act.wait_ge(right_ready[k], n + 1)
                    act.wait_ge(right_used[k], n + 1)
                    nc.scalar.activation(right[:, half, :], right_ps[:, half, :], ACT.Tanh).then_inc(right_out[k], 1)

                with act.Fori(0, HOPS) as hop:
                    n, m = act.snap(hop * (all_bodies + 1)), act.snap(hop * (all_bodies + 2))
                    proj.scalar(act, hop)
                    move_kinds(m)
                    move_kinds(m + 1)
                    for k in range(HALVES):
                        move_messages(n, k)
                        tanh(n, k)
                    with act.Fori(0, all_bodies) as i:
                        move_kinds(m + i + 2)
                        move_messages(n + i + 1, 0)
                        tanh(n + i + 1, 0)
                        soft.exponentials(act, hop * all_bodies + i)
                        move_messages(n + i + 1, 1)
                        tanh(n + i + 1, 1)
                    act.wait_ge(sums_ready, hop + 1)
                    nc.scalar.activation(col[:, 1, :], col[:, 0, :], ACT.Sqrt).then_inc(norms_ready, 1)

            @block.vector
            def _(v):
                V = nc.vector
                all_bodies = stream.total(v)
                proj.open(v)
                for k in range(HALVES):
                    v.sem_inc(stream.land_free[k], 1)
                    v.sem_inc(right_used[k], 1)
                V.tensor_copy(res[:, :, :], h[:, :, :])
                v.wait_ge(weights_in, 64)
                V.memset(parts[:, :, :, :], 0.0)
                V.tensor_copy(rest[:, :], relation[:, :])
                v.drain()
                for t in range(3):
                    for k in range(2):
                        rows = slice(k * KINDS, (k + 1) * KINDS)
                        V.tensor_copy(parts[rows, t, k, :], rest[rows, :])
                    v.drain()
                    for k in range(2):
                        rows = slice(k * KINDS, (k + 1) * KINDS)
                        V.tensor_tensor(rest[rows, :], rest[rows, :], parts[rows, t, k, :], ALU.subtract)
                    v.drain()
                V.tensor_scalar(col[:, 0, :], c.degs[0][:, :], 1.0, None, ALU.max)
                V.tensor_scalar(col[:, 2, :], c.degs[0][:, :], 0.0, None, ALU.is_gt)
                v.drain()
                V.reciprocal(col[:, 1, :], col[:, 0, :])
                v.drain()
                V.tensor_tensor(share[:, :], col[:, 1, :], col[:, 2, :], ALU.mult)
                v.drain()
                v.sem_inc(proj.source_ready, 1)

                def kinds(m):
                    for k in range(HALVES):
                        v.wait_ge(kind_in[k], m * 16 + 16)
                        v.wait_ge(hotT_moved[k], m + 1)
                        V.tensor_tensor(hot[:, k, :, :], spread(c.iota_row[:, 0:KINDS], [P, H, KINDS], 1),
                                        kind[:, k, :, 1:2].to_broadcast([P, H, KINDS]),
                                        ALU.is_equal).then_inc(hot_ready[k], 1)

                def free_kinds(m):
                    for k in range(HALVES):
                        v.wait_ge(hot_ready[k], m + 1)
                        v.sem_inc(kind_free[k], 1)

                def messages(n, m, k):
                    half = slice(k * H, (k + 1) * H)
                    v.wait_ge(stream.landed[k], n * (16 * H) + 16 * H)
                    v.wait_ge(rel_ready[k], m + 1)
                    v.wait_ge(kept_ready[k], n + 1)
                    V.tensor_tensor(message[:, half, :], stream.land[:, half, :], rel_ps[:, half, :],
                                    ALU.mult).then_inc(message_ready[k], 1)

                def free_rows(n, k):
                    v.wait_ge(message_ready[k], n + 1)
                    v.sem_inc(stream.land_free[k], 1)

                with v.Fori(0, HOPS) as hop:
                    def take(b, products):
                        return V.tensor_copy(left[:, bass.ds(b, proj.group), :], products)

                    proj.vector(v, hop, take)
                    v.wait_ge(stream.table_in, hop * z.stored + z.stored)
                    for j in range(2):
                        kinds(hop * (all_bodies + 2) + j)
                        free_kinds(hop * (all_bodies + 2) + j)
                    for k in range(HALVES):
                        messages(hop * (all_bodies + 1), hop * (all_bodies + 2), k)
                        free_rows(hop * (all_bodies + 1), k)
                    with v.Fori(0, NB) as b:
                        many, first = stream.block(v, b)
                        n0 = v.snap(hop * (all_bodies + 1) + first)
                        m0 = v.snap(hop * (all_bodies + 2) + first)
                        soft.begin(c.degs[0][:, bass.ds(b, 1)])
                        V.memset(total[:, :], 0.0)
                        V.tensor_copy(left_now[:, :], left[:, bass.ds(b, 1), :].rearrange("p a d -> p (a d)"))
                        v.drain()
                        with v.Fori(0, many) as i:
                            n = v.snap(n0 + i)
                            m = v.snap(m0 + i)
                            kinds(m + 2)
                            messages(n + 1, m + 1, 0)
                            soft.mark(c.iota_row)
                            for k in range(HALVES):
                                v.wait_ge(right_out[k], n + 2)
                                for s in range(k * H, (k + 1) * H):
                                    last = V.tensor_tensor_reduce(product[:, s, :], right[:, s, :], left_now[:, :],
                                                                  op0=ALU.mult, op1=ALU.add, scale=1.0, scalar=0.0,
                                                                  accum_out=soft.score[:, s, :])
                                last.then_inc(right_used[k], 1)
                                if k == 0:
                                    free_kinds(m + 2)
                                    free_rows(n + 1, 0)
                            v.drain()
                            soft.scores(v)
                            messages(n + 1, m + 1, 1)
                            for k in range(HALVES):
                                v.wait_ge(kept_ready[k], n + 2)
                            soft.weigh(v, hop * all_bodies + first + i,
                                       kept[:, bass.ds(n % 2, 1), :, :].rearrange("p a s d -> p (a s) d"),
                                       product, total, part, D, lambda: free_rows(n + 1, 1))
                            v.drain()
                        V.reciprocal(scale[:, :], soft.denom[:, :])
                        v.drain()
                        V.tensor_tensor(scale[:, :], scale[:, :], share[:, bass.ds(b, 1)], ALU.mult)
                        v.drain()
                        V.tensor_scalar(res[:, bass.ds(b, 1), :].rearrange("p a d -> p (a d)"), total[:, :],
                                        scale[:, 0:1], None, ALU.mult)
                        v.drain()
                    V.tensor_tensor(work[:, :, :], res[:, :, :], res[:, :, :], ALU.mult)
                    V.tensor_tensor(x[:, :, :], x[:, :, :], h[:, :, :], ALU.add)
                    v.drain()
                    V.tensor_reduce(col[:, 0, :], work[:, :, :], AX.X, ALU.add).then_inc(sums_ready, 1)
                    v.wait_ge(norms_ready, hop + 1)
                    V.tensor_scalar(col[:, 2, :], col[:, 1, :], 1e-12, None, ALU.max)
                    v.drain()
                    V.reciprocal(col[:, 3, :], col[:, 2, :])
                    v.drain()
                    V.tensor_tensor(res[:, :, :], res[:, :, :], spread(col[:, 3, :], [P, NB, D], 2), ALU.mult)
                    v.drain()
                    V.tensor_tensor(x[:, :, :], x[:, :, :], res[:, :, :], ALU.add)
                    v.drain()
                    for k in range(HALVES):
                        v.wait_ge(right_out[k], hop * (all_bodies + 1) + all_bodies + 2)
                        v.sem_inc(right_used[k], 1)
                    v.sem_inc(proj.source_ready, 1)


def graph_attention(nc, top, z, c, a, x, h, res, work):
    NB, LAYERS, HEADS = z.blocks, 3, 4
    C = D // HEADS
    W = D + HEADS
    with ExitStack() as ctx:
        def sb(name, shape, dt=F32):
            return ctx.enter_context(nc.sbuf_tensor(name, shape, dt))

        def sem(name):
            return top.sem(name)

        w = sb("gat_w", [P, LAYERS, 2, D])
        att = sb("gat_att", [P, LAYERS, 2, D])
        bias = sb("gat_bias", [P, LAYERS, D])
        floor = sb("gat_floor", [P, LAYERS])
        rows = sb("gat_rows", [P, NB, W])
        own = sb("gat_own", [P, NB, HEADS])
        scaled = sb("gat_scaled", [P, 5, 2, D])
        body_rows = sb("gat_body_rows", [P, S, W])
        weighed = sb("gat_weighed", [P, S, D])
        raw = sb("gat_raw", [P, S, HEADS])
        total, part = sb("gat_total", [P, D]), sb("gat_part", [P, D])
        denom, inverse = sb("gat_denom", [P, HEADS]), sb("gat_inverse", [P, HEADS])
        stream = Stream(nc, ctx, top, z, "l1", c.ells[1], c.plans[1], W)
        soft = Softmax(nc, ctx, top, "l1", HEADS)
        proj = Projection(nc, ctx, top, z, "gat", 1, 2 * D)
        weights_in = sem("l1_weights_in")
        rows_ready = sem("l1_rows_ready")
        copied = [sem(f"l1_copied{k}") for k in range(HALVES)]
        rows_used = sem("l1_rows_used")

        with nc.Block() as block:

            @block.sync
            def _(sp):
                for n in range(2):
                    sp.dma_start(w[:, :, n, :], a["gat_w"][n].rearrange("l k n -> k l n")).then_inc(weights_in, 16)
                    sp.dma_start(att[:, :, n, :], a["gat_att"][n].rearrange("(a l) n -> a l n", a=1)
                                 .to_broadcast([P, LAYERS, D])).then_inc(weights_in, 16)
                sp.dma_start(bias[:, :, :], a["gat_b"].rearrange("(a l) n -> a l n", a=1)
                             .to_broadcast([P, LAYERS, D])).then_inc(weights_in, 16)
                all_bodies = stream.total(sp)
                with sp.Fori(0, LAYERS) as layer:
                    sp.wait_ge(rows_ready, layer + 1)
                    stream.load_all(sp, layer, all_bodies)

            @block.gpsimd
            def _(pool):
                all_bodies = stream.total(pool)
                with pool.Fori(0, LAYERS) as layer:
                    stand(pool, stream.turns, rows_ready, layer + 1)
                    scatter_rows(pool, z, c.perms[1], c.table_w, rows, stream.table_in)
                    stand(pool, stream.turns, stream.table_in, layer * z.stored + z.stored)
                    with pool.Fori(0, all_bodies) as body:
                        for k in range(HALVES):
                            stream.gather(pool, layer * all_bodies + body, k, [(c.table_w, 0, stream.land)])

            @block.tensor
            def _(pe):
                pe.wait_ge(weights_in, 80)
                with pe.Fori(0, LAYERS) as layer:
                    proj.tensor(pe, layer, lambda b, _: res[:, b, :],
                                lambda _: w[:, bass.ds(layer, 1), :, :].rearrange("p a t d -> p (a t d)"),
                                c.ident[:, :])

            @block.scalar
            def _(act):
                all_bodies = stream.total(act)
                with act.Fori(0, LAYERS) as layer:
                    proj.scalar(act, layer)
                    with act.Fori(0, all_bodies) as body:
                        n = layer * all_bodies + body
                        act.wait_ge(rows_used, n + 1)
                        for k in range(HALVES):
                            act.wait_ge(stream.landed[k], n * (16 * H) + 16 * H)
                            nc.scalar.copy(body_rows[:, k * H:(k + 1) * H, :],
                                           stream.land[:, k * H:(k + 1) * H, :]).then_inc(copied[k], 1)
                            act.wait_ge(copied[k], n + 1)
                            act.sem_inc(stream.land_free[k], 1)
                        soft.exponentials(act, n)

            @block.vector
            def _(v):
                V = nc.vector
                all_bodies = stream.total(v)
                proj.open(v)
                for k in range(HALVES):
                    v.sem_inc(stream.land_free[k], 1)
                v.sem_inc(rows_used, 1)
                V.memset(floor[:, 0:LAYERS - 1], 0.0)
                V.memset(floor[:, LAYERS - 1:LAYERS], -3.0e38)
                V.tensor_copy(res[:, :, :], h[:, :, :])
                v.wait_ge(weights_in, 80)
                v.drain()
                v.sem_inc(proj.source_ready, 1)
                with v.Fori(0, LAYERS) as layer:
                    def take(b, products):
                        at = bass.ds(b, proj.group)
                        both = products.rearrange("p g (t d) -> p g t d", t=2)
                        V.tensor_tensor(scaled[:, :, :, :].rearrange("p g t d -> p g (t d)"), products,
                                        att[:, bass.ds(layer, 1), :, :].rearrange("p a t d -> p a (t d)")
                                        .to_broadcast([P, proj.group, 2 * D]), ALU.mult)
                        last = V.tensor_copy(rows[:, at, 0:D], both[:, :, 0, :])
                        v.drain()
                        V.tensor_reduce(rows[:, at, D:W], scaled[:, :, 0, :].rearrange("p g (h c) -> p g h c", c=C),
                                        AX.X, ALU.add)
                        V.tensor_reduce(own[:, at, :], scaled[:, :, 1, :].rearrange("p g (h c) -> p g h c", c=C),
                                        AX.X, ALU.add)
                        v.drain()
                        return V.memset(part[:, 0:1], 0.0)

                    proj.vector(v, layer, take)
                    v.sem_inc(rows_ready, 1)
                    with v.Fori(0, NB) as b:
                        many, first = stream.block(v, b)
                        soft.begin(c.degs[1][:, bass.ds(b, 1)])
                        V.memset(total[:, :], 0.0)
                        v.drain()
                        with v.Fori(0, many) as i:
                            n = layer * all_bodies + first + i
                            soft.mark(c.iota_row)
                            for k in range(HALVES):
                                v.wait_ge(copied[k], n + 1)
                            V.tensor_tensor(raw[:, :, :], body_rows[:, :, D:W],
                                            own[:, bass.ds(b, 1), :].to_broadcast([P, S, HEADS]), ALU.add)
                            v.drain()
                            V.scalar_tensor_tensor(out=soft.score[:, :, :], in0=raw[:, :, :], scalar=0.2,
                                                   in1=raw[:, :, :], op0=ALU.mult, op1=ALU.max)
                            v.drain()
                            soft.scores(v)
                            soft.weigh(v, n, body_rows[:, :, 0:D], weighed, total, part, D)
                            v.drain()
                            v.sem_inc(rows_used, 1)
                        V.tensor_scalar(denom[:, :], soft.denom[:, :], 1e-16, None, ALU.add)
                        v.drain()
                        V.reciprocal(inverse[:, :], denom[:, :])
                        v.drain()
                        V.tensor_tensor(part[:, :].rearrange("p (h c) -> p h c", c=C),
                                        total[:, :].rearrange("p (h c) -> p h c", c=C),
                                        spread(inverse[:, :], [P, HEADS, C], 2), ALU.mult)
                        v.drain()
                        V.tensor_tensor(part[:, :], part[:, :],
                                        bias[:, bass.ds(layer, 1), :].rearrange("p a d -> p (a d)"), ALU.add)
                        v.drain()
                        V.tensor_scalar(res[:, bass.ds(b, 1), :].rearrange("p a d -> p (a d)"), part[:, :],
                                        floor[:, bass.ds(layer, 1)], None, ALU.max)
                        v.drain()
                    v.wait_ge(stream.table_in, layer * z.stored + z.stored)
                    v.sem_inc(proj.source_ready, 1)
                V.tensor_tensor(x[:, :, :], x[:, :, :], res[:, :, :], ALU.add)
                v.drain()


def sum_neighbours(nc, top, z, c, name, rows, res):
    NB = z.blocks
    with ExitStack() as ctx:
        total = ctx.enter_context(nc.sbuf_tensor(f"{name}_total", [P, D], F32))
        part = ctx.enter_context(nc.sbuf_tensor(f"{name}_part", [P, HALVES, D], F32))
        stream = Stream(nc, ctx, top, z, name, c.ells[1], c.plans[1], D)
        with nc.Block() as block:

            @block.sync
            def _(sp):
                all_bodies = stream.total(sp)
                stream.load_all(sp, 0, all_bodies)

            @block.gpsimd
            def _(pool):
                all_bodies = stream.total(pool)
                scatter_rows(pool, z, c.perms[1], c.table, rows, stream.table_in)
                pool.wait_ge(stream.table_in, z.stored)
                with pool.Fori(0, all_bodies) as body:
                    for k in range(HALVES):
                        stream.gather(pool, body, k, [(c.table, 0, stream.land)])

            @block.vector
            def _(v):
                V = nc.vector
                for k in range(HALVES):
                    v.sem_inc(stream.land_free[k], 1)
                v.wait_ge(stream.table_in, z.stored)
                with v.Fori(0, NB) as b:
                    many, first = stream.block(v, b)
                    V.memset(total[:, :], 0.0)
                    with v.Fori(0, many) as i:
                        n = first + i
                        for k in range(HALVES):
                            v.wait_ge(stream.landed[k], n * (16 * H) + 16 * H)
                            V.tensor_reduce(part[:, k, :], stream.land[:, k * H:(k + 1) * H, :]
                                            .rearrange("p s d -> p d s"), AX.X, ALU.add)
                            v.drain()
                            v.sem_inc(stream.land_free[k], 1)
                            V.tensor_tensor(total[:, :], total[:, :], part[:, k, :], ALU.add)
                            v.drain()
                    V.tensor_copy(res[:, bass.ds(b, 1), :].rearrange("p a d -> p (a d)"), total[:, :])
                    v.drain()


def project(nc, top, z, c, name, chunks, width, weights_in, count, source, weights, target, finish, exps=0):
    with ExitStack() as ctx:
        proj = Projection(nc, ctx, top, z, name, chunks, width)
        with nc.Block() as block:

            @block.tensor
            def _(pe):
                pe.wait_ge(weights_in, count)
                pe.sem_inc(proj.source_ready, 1)
                proj.tensor(pe, 0, source, weights, c.ident[:, :])

            @block.scalar
            def _(act):
                proj.scalar(act, 0)

            @block.vector
            def _(v):
                proj.open(v)
                v.wait_ge(weights_in, count)

                def take(b, products):
                    return nc.vector.tensor_copy(target[:, bass.ds(b, proj.group), :], products)

                proj.vector(v, 0, take)
                finish(v)


def graph_convolution(nc, top, z, c, a, x, h, res, work):
    NB = z.blocks
    WIDE = 2 * D
    with ExitStack() as ctx:
        def sb(name, shape, dt=F32):
            return ctx.enter_context(nc.sbuf_tensor(name, shape, dt))

        def sem(name):
            return top.sem(name)

        w1, w2 = sb("w1", [P, WIDE]), sb("w2", [P, 2, D])
        fc1, fc2 = sb("fc1", [P, D]), sb("fc2", [P, D])
        b1, b2, fb1, fb2 = sb("b1", [P, WIDE]), sb("b2", [P, D]), sb("fb1", [P, D]), sb("fb2", [P, D])
        norm_src, norm_dst = sb("norm_src", [P, NB]), sb("norm_dst", [P, NB])
        out_degree = sb("out_degree", [P, NB])
        degree_in = sem("l2_degree_in")
        col = sb("gcn_col", [P, 4, NB])
        hidden = sb("hidden", [P, NB, WIDE])
        weights_in = sem("l2_weights_in")
        counts_ready, roots_ready = sem("l2_counts_ready"), sem("l2_roots_ready")
        exp_in, exp_out = sem("l2_exp_in"), sem("l2_exp_out")
        loads = [(w1[:, :], a["w1"]), (w2[:, :, :], a["w2"].rearrange("(c k) n -> k c n", k=P)), (fc1[:, :], a["fc1"]),
                 (fc2[:, :], a["fc2"])]
        loads += [(to[:, :], a[k].rearrange("(a n) -> a n", a=1).to_broadcast([P, to.shape[1]]))
                  for to, k in ((b1, "b1"), (b2, "b2"), (fb1, "fb1"), (fb2, "fb2"))]
        arrived = 16 * len(loads)

        with nc.Block() as block:
            @block.sync
            def _(sp):
                for to, of in loads:
                    sp.dma_start(to, of).then_inc(weights_in, 16)

            @block.gpsimd
            def _(pool):
                gather_rows(pool, z, c.perms[1], c.degree_dram[0], out_degree[:, :].unsqueeze(2), degree_in)

            @block.vector
            def _(v):
                V = nc.vector
                v.wait_ge(degree_in, z.stored)
                V.tensor_scalar(col[:, 0, :], out_degree[:, :], 1.0, None, ALU.max)
                V.tensor_scalar(col[:, 1, :], c.degs[1][:, :], 1.0, None, ALU.max).then_inc(counts_ready, 1)
                v.wait_ge(roots_ready, 1)
                V.reciprocal(col[:, 0:2, :], col[:, 2:4, :])
                v.drain()
                V.scalar_tensor_tensor(out=norm_src[:, :], in0=out_degree[:, :], scalar=0.0, in1=col[:, 0, :],
                                       op0=ALU.is_gt, op1=ALU.mult)
                V.scalar_tensor_tensor(out=norm_dst[:, :], in0=c.degs[1][:, :], scalar=0.0, in1=col[:, 1, :],
                                       op0=ALU.is_gt, op1=ALU.mult)
                v.drain()
                V.tensor_tensor(work[:, :, :], h[:, :, :], spread(norm_src[:, :], [P, NB, D], 2), ALU.mult)
                v.drain()

            @block.scalar
            def _(act):
                act.wait_ge(counts_ready, 1)
                nc.scalar.activation(col[:, 2:4, :], col[:, 0:2, :], ACT.Sqrt).then_inc(roots_ready, 1)

        sum_neighbours(nc, top, z, c, "gcn1", work, res)

        def block_of(t):
            return lambda b, k: t[:, b, k * P:(k + 1) * P]

        def scale_bias(v, t, scale, bias, width):
            V, wide = nc.vector, [P, NB, width]
            if scale is not None:
                V.tensor_tensor(t[:, :, :], t[:, :, :], spread(scale[:, :], wide, 2), ALU.mult)
                v.drain()
            V.tensor_tensor(t[:, :, :], t[:, :, :], spread(bias[:, :], wide, 1), ALU.add)
            v.drain()

        def finish_first(v):
            scale_bias(v, hidden, norm_dst, b1, WIDE)
            nc.vector.tensor_scalar(hidden[:, :, :], hidden[:, :, :], 0.0, None, ALU.max)
            v.drain()
            nc.vector.tensor_tensor(hidden[:, :, :], hidden[:, :, :], spread(norm_src[:, :], [P, NB, WIDE], 2),
                                    ALU.mult)
            v.drain()

        project(nc, top, z, c, "gcn_w1", 1, WIDE, weights_in, arrived, block_of(res), lambda k: w1[:, :],
                hidden, finish_first)
        project(nc, top, z, c, "gcn_w2", 2, D, weights_in, arrived, block_of(hidden), lambda k: w2[:, k, :],
                work, lambda v: None)
        sum_neighbours(nc, top, z, c, "gcn2", work, res)

        with nc.Block() as block:
            @block.vector
            def _(v):
                scale_bias(v, res, norm_dst, b2, D)
                nc.vector.tensor_scalar(res[:, :, :], res[:, :, :], 0.0, None, ALU.max)
                v.drain()

        negative = hidden[:, :, 0:D]

        def finish_elu(v):
            scale_bias(v, work, None, fb1, D)
            nc.vector.tensor_scalar(negative, work[:, :, :], 0.0, None, ALU.min)
            v.drain()

        project(nc, top, z, c, "fc1_p", 1, D, weights_in, arrived, block_of(res), lambda k: fc1[:, :],
                work, finish_elu)
        with nc.Block() as block:
            @block.scalar
            def _(act):
                nc.scalar.activation(negative, negative, ACT.Exp).then_inc(exp_out, 1)

            @block.vector
            def _(v):
                V = nc.vector
                V.tensor_scalar(work[:, :, :], work[:, :, :], 0.0, -1.0, ALU.max, ALU.add)
                v.wait_ge(exp_out, 1)
                v.drain()
                V.tensor_tensor(work[:, :, :], work[:, :, :], negative, ALU.add)
                v.drain()

        def finish_out(v):
            scale_bias(v, res, None, fb2, D)
            nc.vector.tensor_tensor(x[:, :, :], x[:, :, :], res[:, :, :], ALU.add)
            v.drain()

        project(nc, top, z, c, "fc2_p", 1, D, weights_in, arrived, block_of(work), lambda k: fc2[:, :],
                res, finish_out)


def composed_attention(nc, top, z, c, a, x, h, res, work, out):
    NB = z.blocks
    with ExitStack() as ctx:
        def sb(name, shape, dt=F32):
            return ctx.enter_context(nc.sbuf_tensor(name, shape, dt))

        def sem(name):
            return top.sem(name)

        neigh_w = sb("neigh_w", [P, D])
        rel_land = sb("rel_land", [P, S, D])
        comp = sb("comp", [P, S, D])
        product = sb("l3_product", [P, S, D])
        total, part = sb("l3_total", [P, D]), sb("l3_sum", [P, D])
        scale, present = sb("l3_scale", [P, 1]), sb("l3_present", [P, NB])
        stream = Stream(nc, ctx, top, z, "l3", c.ells[1], c.plans[1], D, sources=2)
        soft = Softmax(nc, ctx, top, "l3", 1)
        weights_in, out_done = sem("l3_weights_in"), sem("out_done")
        tanh_out, final, x_out = sem("tanh_out"), sem("final"), sem("x_out")

        with nc.Block() as block:

            @block.sync
            def _(sp):
                sp.dma_start(neigh_w[:, :], a["neigh_w"]).then_inc(weights_in, 16)
                all_bodies = stream.total(sp)
                stream.load_all(sp, 0, all_bodies)

            @block.gpsimd
            def _(pool):
                all_bodies = stream.total(pool)
                scatter_rows(pool, z, c.perms[1], c.table, h, stream.table_in)
                pool.wait_ge(stream.table_in, z.stored)
                with pool.Fori(0, all_bodies) as body:
                    for k in range(HALVES):
                        stream.gather(pool, body, k, [(c.table, 0, stream.land), (a["rel_emb"], 1, rel_land)])

            @block.scalar
            def _(act):
                all_bodies = stream.total(act)
                with act.Fori(0, all_bodies) as body:
                    soft.exponentials(act, body)

            @block.vector
            def _(v):
                V = nc.vector
                for k in range(HALVES):
                    v.sem_inc(stream.land_free[k], 1)
                V.tensor_scalar(present[:, :], c.degs[1][:, :], 0.0, None, ALU.is_gt)
                v.wait_ge(stream.table_in, z.stored)
                v.wait_ge(weights_in, 16)
                with v.Fori(0, NB) as b:
                    many, first = stream.block(v, b)
                    soft.begin(c.degs[1][:, bass.ds(b, 1)])
                    V.memset(total[:, :], 0.0)
                    v.drain()
                    with v.Fori(0, many) as i:
                        n = first + i
                        soft.mark(c.iota_row)
                        for k in range(HALVES):
                            half = slice(k * H, (k + 1) * H)
                            v.wait_ge(stream.landed[k], n * (32 * H) + 32 * H)
                            V.tensor_tensor(comp[:, half, :], stream.land[:, half, :], rel_land[:, half, :], ALU.add)
                            v.drain()
                            v.sem_inc(stream.land_free[k], 1)
                            V.tensor_tensor(product[:, half, :], comp[:, half, :],
                                            h[:, bass.ds(b, 1), :].to_broadcast([P, H, D]), ALU.mult)
                        v.drain()
                        V.tensor_reduce(soft.score[:, :, :].rearrange("p s h -> p (s h)"),
                                        product[:, :, :], AX.X, ALU.add)
                        v.drain()
                        soft.scores(v)
                        soft.weigh(v, n, comp[:, :, :], product, total, part, D)
                        v.drain()
                    V.reciprocal(scale[:, :], soft.denom[:, :])
                    v.drain()
                    V.tensor_tensor(scale[:, :], scale[:, :], present[:, bass.ds(b, 1)], ALU.mult)
                    v.drain()
                    V.tensor_scalar(res[:, bass.ds(b, 1), :].rearrange("p a d -> p (a d)"), total[:, :],
                                    scale[:, 0:1], None, ALU.mult)
                    v.drain()

        project(nc, top, z, c, "neigh_p", 1, D, weights_in, 16,
                lambda b, _: res[:, b, :],
                lambda _: neigh_w[:, :], work, lambda v: None)
        with nc.Block() as block:
            @block.scalar
            def _(act):
                nc.scalar.activation(work[:, :, :], work[:, :, :], ACT.Tanh).then_inc(tanh_out, 1)

            @block.vector
            def _(v):
                v.wait_ge(tanh_out, 1)
                nc.vector.tensor_tensor(x[:, :, :], x[:, :, :], work[:, :, :], ALU.add).then_inc(final, 1)

            @block.gpsimd
            def _(pool):
                pool.wait_ge(final, 1)
                scatter_rows(pool, z, c.perms[1], c.table, x, x_out)

            @block.sync
            def _(sp):
                sp.wait_ge(x_out, z.stored)
                sp.dma_start(out[:, :], c.table[0:z.nodes, :]).then_inc(out_done, 16)
                sp.wait_ge(out_done, 16)


class Common:
    pass


def reorder(nc, top, z, name, source, to, x, table=None, of=None):
    out, back = top.sem(f"{name}_out"), top.sem(f"{name}_back")
    with nc.Block() as block:
        @block.gpsimd
        def _(pool):
            if of is not None:
                scatter_rows(pool, z, of, source, x, out)
                pool.wait_ge(out, z.stored)
            gather_rows(pool, z, to, source, x, back)
            pool.wait_ge(back, z.stored)


def program(nc, z, a, out):
    with ExitStack() as ctx:
        def sb(name, shape, dt=F32):
            return ctx.enter_context(nc.sbuf_tensor(name, shape, dt))

        def dram(name, shape, dt=F32):
            return nc.dram_tensor(name, shape, dt, kind="Internal").ap()

        NB = z.blocks
        iota_i = sb("iota_i", [P, P], I32)
        iota_ci = sb("iota_ci", [P, 1], I32)
        iota_row, iota_col, iota_rb = sb("iota_row", [P, P]), sb("iota_col", [P, 1]), sb("iota_rb", [P, P], BF16)
        before, zero = sb("before", [P, H, P], BF16), sb("zero", [P, D + 4])
        earlier = sb("earlier", [P, P])
        c = Common()
        c.iota_row = iota_row
        c.ident, c.ident_b = sb("ident", [P, P]), sb("ident_b", [P, P], BF16)
        c.natural_deg = sb("natural_deg", [P, 2, NB])
        c.degs = [sb(f"deg{q}", [P, NB]) for q in range(2)]
        c.plans = [sb(f"plan{q}", [P, 2 * NB + 2], I32) for q in range(2)]
        c.perms = [sb(f"perm{q}", [P, NB, 2], I32) for q in range(2)]
        c.ells = [dram(f"ell{q}", [(z.bodies + 2 * BLANKS) * S * P, 2], I32) for q in range(2)]
        c.perm_dram = [dram(f"perm_dram{q}", [z.rows, 2], I32) for q in range(2)]
        c.degree_dram = [dram(f"degree_dram{q}", [z.rows, 1]) for q in range(2)]
        c.order_dram = dram("order_dram", [z.rows, 1])
        c.table, c.table_w = dram("table", [z.rows + P, D]), dram("table_w", [z.rows + P, D + 4])
        consts_i = ctx.enter_context(nc.semaphore("consts_i"))
        consts_f = ctx.enter_context(nc.semaphore("consts_f"))
        blank_rows = ctx.enter_context(nc.semaphore("blank_rows"))

        with nc.Block() as block:
            @block.gpsimd
            def _(pool):
                nc.gpsimd.iota(iota_i[:, :], pattern=[[1, P]], base=0, channel_multiplier=0).then_inc(consts_i, 1)
                nc.gpsimd.iota(iota_ci[:, :], pattern=[[0, 1]], base=0, channel_multiplier=1).then_inc(consts_i, 1)

            @block.sync
            def _(sp):
                sp.wait_ge(consts_f, 1)
                sp.dma_start(c.table[z.rows:z.rows + P, :], zero[:, 0:D]).then_inc(blank_rows, 16)
                sp.dma_start(c.table_w[z.rows:z.rows + P, :], zero[:, :]).then_inc(blank_rows, 16)
                sp.wait_ge(blank_rows, 32)

            @block.vector
            def _(v):
                nc.vector.memset(zero[:, :], 0.0).then_inc(consts_f, 1)
                v.wait_ge(consts_i, 2)
                nc.vector.tensor_copy(iota_row[:, :], iota_i[:, :]).then_inc(consts_f, 1)
                nc.vector.tensor_copy(iota_rb[:, :], iota_i[:, :]).then_inc(consts_f, 1)
                nc.vector.tensor_copy(iota_col[:, :], iota_ci[:, :]).then_inc(consts_f, 1)
                v.wait_ge(consts_f, 4)
                nc.vector.tensor_scalar(earlier[:, :], iota_row[:, :], iota_col[:, 0:1], None, ALU.is_lt)
                nc.vector.tensor_scalar(c.ident[:, :], iota_row[:, :], iota_col[:, 0:1], None, ALU.is_equal)
                v.drain()
                nc.vector.tensor_scalar(before[:, :, :], spread(earlier[:, :], [P, H, P], 1),
                                        float(z.bits + 1), float(-2 * z.bits), ALU.mult, ALU.add)
                nc.vector.tensor_copy(c.ident_b[:, :], c.ident[:, :])
                v.drain()

        with Semaphores(nc) as top, ExitStack() as grouping:
            group_edges(nc, grouping, top, z, a, c, zero, (iota_row, iota_rb, iota_col, c.ident_b, before))

        x = sb("x", [P, NB, D])
        h, res, work = sb("h", [P, NB, D]), sb("res", [P, NB, D]), sb("work", [P, NB, D])
        col = sb("col", [P, 4, NB])
        with Semaphores(nc) as top:
            reorder(nc, top, z, "x0", a["x"], c.perms[0], x)
            normalize(nc, top, z, "n0", x, h, work, col)
        with Semaphores(nc) as top:
            attention_over_relations(nc, top, z, c, a, x, h, res, work)
        with Semaphores(nc) as top:
            reorder(nc, top, z, "x1", c.table, c.perms[1], x, of=c.perms[0])
            normalize(nc, top, z, "n1", x, h, work, col)
        with Semaphores(nc) as top:
            graph_attention(nc, top, z, c, a, x, h, res, work)
        with Semaphores(nc) as top:
            normalize(nc, top, z, "n2", x, h, work, col)
            graph_convolution(nc, top, z, c, a, x, h, res, work)
        with Semaphores(nc) as top:
            normalize(nc, top, z, "n3", x, h, work, col)
            composed_attention(nc, top, z, c, a, x, h, res, work, out)


NAMES = {"x": "x", "L0_gnn_edge_emb": "edge_emb", "L0_gnn_q_w": "q_w", "L0_gnn_k_w": "k_w", "L1_gnn_b": "gat_b",
         "L2_gnn_W1": "w1", "L2_gnn_b1": "b1", "L2_gnn_W2": "w2", "L2_gnn_b2": "b2", "L2_gnn_fc1_w": "fc1",
         "L2_gnn_fc1_b": "fb1", "L2_gnn_fc2_w": "fc2", "L2_gnn_fc2_b": "fb2", "L3_gnn_rel_emb": "rel_emb",
         "L3_gnn_neigh_w": "neigh_w"}


def kernel(**inputs):
    import numpy as _np
    import concourse.bacc as _bacc
    from concourse import mybir as _mybir
    from concourse.bass_utils import run_bass_kernel_spmd as _run

    nodes, edges = inputs["x"].shape[0], inputs["src"].shape[0]
    tiles_at_once = 2 * S * CHUNKS
    tiles = -(-edges // (P * tiles_at_once)) * tiles_at_once
    z = Shapes(nodes, tiles)
    fill = tiles * P - edges
    spare = (nodes + _np.arange(fill) % (z.rows - nodes)).astype(_np.int32)
    dummy, none = _np.full(fill, z.dummy, _np.int32), _np.zeros(fill, _np.int32)

    def padded(name, tail):
        return _np.concatenate([_np.asarray(inputs[name]), tail])

    arrays = {}
    for k, (key, other, kind) in enumerate((("src", "dst", "edge_type_64"), ("dst", "src", "edge_type_474"))):
        arrays[f"keys{k}"] = _np.ascontiguousarray(padded(key, spare).reshape(tiles, P).T)
        pair = _np.stack([padded(other, dummy), padded(kind, none)], axis=-1)
        arrays[f"payload{k}"] = _np.ascontiguousarray(pair.reshape(tiles, P, 2).transpose(1, 0, 2))
    for name, k in NAMES.items():
        arrays[k] = _np.ascontiguousarray(inputs[name])
    arrays["x"] = _np.concatenate([arrays["x"], _np.zeros((z.rows - nodes, D), _np.float32)])
    layers = inputs["L1_gnn_b"].shape[0]
    arrays["ws"], arrays["wd"] = (_np.ascontiguousarray(inputs[f"L1_gnn_W{k}"]) for k in "sd")
    arrays["att_s"], arrays["att_d"] = (_np.ascontiguousarray(inputs[f"L1_gnn_att_{k}"]).reshape(layers, D)
                                        for k in "sd")

    nc = _bacc.Bacc("TRN2", target_bir_lowering=False, num_devices=1)
    a = {k: nc.dram_tensor(f"in_{k}", v.shape, _mybir.dt.from_np(v.dtype), kind="ExternalInput").ap()
         for k, v in arrays.items()}
    a["gat_w"], a["gat_att"] = (a["ws"], a["wd"]), (a["att_s"], a["att_d"])
    a["key_cols"], a["payloads"] = (a["keys0"], a["keys1"]), (a["payload0"], a["payload1"])
    out = nc.dram_tensor("out_dram", (nodes, D), F32, kind="ExternalOutput").ap()
    program(nc, z, a, out)
    r = _run(nc, [{f"in_{k}": v for k, v in arrays.items()}], core_ids=[0])
    return r.results[0]["out_dram"]
```

```python
from contextlib import ExitStack

import concourse.bass as bass
from concourse import mybir

P = 128
D = 128
S = 8
H = 4
HALVES = S // H
CHUNKS = 17
RING = 4
HALF_BITS = 15
BLANKS = 16

F32 = mybir.dt.float32
BF16 = mybir.dt.bfloat16
I32 = mybir.dt.int32
ALU = mybir.AluOpType
ACT = mybir.ActivationFunctionType
AX = mybir.AxisListType
RMAX = bass.bass_isa.ReduceOp.max
NEG = -1.0e30
ABSENT = 2 * NEG


class Shapes:
    def __init__(self, nodes, tiles):
        self.nodes = nodes
        self.blocks = -(-nodes // P)
        self.rows = self.blocks * P
        self.dummy = self.rows
        self.tiles = tiles
        self.steps = tiles // S
        self.chunks = CHUNKS
        self.stored = 16 * self.blocks
        self.bits = (self.rows - 1).bit_length()
        self.bodies = tiles * P // S + self.blocks
        assert 2 * self.bodies < 1 << HALF_BITS and self.bodies < 1 << 31 - HALF_BITS


def stand(eng, turns, sem, value):
    eng.wait_ge(sem, value)
    eng.sem_inc(turns, 1)


def group_edges(nc, ctx, top, z, a, c, zero, consts):
    NB, TL, ST, CH, BITS = z.blocks, z.tiles, z.steps, z.chunks, z.bits
    CB = ST // CH
    CR = CB * S // (RING * H)
    ROUNDS = CH * CR
    CK = H * BITS
    V = nc.vector
    iota_row, iota_rb, iota_col, ident_b, before = consts
    NV = 11

    def sb(name, shape, dt=F32):
        return ctx.enter_context(nc.sbuf_tensor(name, shape, dt))

    def pb(name, shape, dt=F32):
        return ctx.enter_context(nc.psum_tensor(name, shape, dt))

    def sem(name):
        return top.sem(name)

    count = sb("count", [P, TL + 1, NB])
    key_i = sb("key_i", [P, TL], I32)
    part_i = sb("part_i", [P, TL], I32)
    key_f, lo_f, hi_f = sb("key_f", [P, TL]), sb("lo_f", [P, TL]), sb("hi_f", [P, TL])
    codes = sb("codes", [P, TL, BITS], BF16)
    pay = sb("pay", [P, 2, TL, 2], I32)
    found = sb("found", [P, TL, 2])
    ahead = sb("ahead", [P, TL])
    eighth_i = sb("eighth_i", [P, CB * S], I32)
    eighth = sb("eighth", [P, CB * S])
    position = sb("position", [P, 2, TL], I32)
    lo_hot = sb("lo_hot", [P, HALVES, H, P], BF16)
    hi_hot = sb("hi_hot", [P, HALVES, H, NB], BF16)
    loT = sb("loT", [P, HALVES, H, P])
    code_at = sb("code_at", [P, HALVES, H, BITS], BF16)
    codeT = sb("codeT", [CK, HALVES, P], BF16)
    diag = sb("diag", [CK, HALVES, H, P], BF16)
    block_mask = sb("block_mask", [CK, H])
    block_end = sb("block_end", [CK, H])
    matched_at = sb("matched_at", [P, HALVES, H, P], BF16)
    within = sb("within", [P, HALVES, H])
    hi_sel = sb("hi_sel", [P, HALVES, H, NB])
    looked_in = sb("looked_in", [P, HALVES, H, 2, NB])
    picked = sb("picked", [P, HALVES, H, 2, NB])
    place = sb("place", [P, NB])
    order = sb("order", [P, NB])
    order_less = sb("order_less", [P, NB])
    order_row = sb("order_row", [P, z.rows])
    above_v = sb("above_v", [P, z.rows], BF16)
    above_a = sb("above_a", [P, z.rows], BF16)
    rank = sb("rank", [P, NB])
    rank_i = sb("rank_i", [P, NB], I32)
    rank_lo_i = sb("rank_lo_i", [P, NB], I32)
    rank_lo, rank_hi = sb("rank_lo", [P, NB]), sb("rank_hi", [P, NB])
    node_f = sb("node_f", [P, NB])
    pairs = sb("pairs", [P, NB, 2], I32)
    block_hot = sb("block_hot", [P, NB, NB])
    most = sb("most", [P, NB])
    nb_i, halves_i = sb("nb_i", [P, NB], I32), sb("halves_i", [P, NB], I32)
    nb_f, end_f, base_f = sb("nb_f", [P, NB]), sb("end_f", [P, NB]), sb("base_f", [P, NB])
    full_f, second_f = sb("full_f", [P, NB]), sb("second_f", [P, NB])
    blank = sb("blank", [P, BLANKS * S, 2], I32)
    stage_at = sb("stage_at", [P, RING, H], I32)
    stage_pay = sb("stage_pay", [P, RING, H, 2], I32)
    counts_ps = [pb(f"counts_ps{h}", [P, H, NB]) for h in range(HALVES)]
    turned_ps = [pb(f"turned_ps{h}", [P, H + 1, P], BF16) for h in range(HALVES)]
    looked_ps = [pb(f"looked_ps{h}", [P, H, 2, NB]) for h in range(HALVES)]
    match_ps = [pb(f"match_ps{h}", [P, H, P]) for h in range(HALVES)]

    def pair(name):
        return [sem(f"{name}{h}") for h in range(HALVES)]

    key_in, pay_in, key_read = sem("key_in"), sem("pay_in"), sem("key_read")
    hots_ready, counts_ready, counts_kept = pair("hots_ready"), pair("counts_ready"), pair("counts_kept")
    dve, act_order = sem("dve_order"), sem("act_order")
    order_ready, order_out, order_in = sem("order_ready"), sem("order_out"), sem("order_in")
    ranked_by_act = sem("ranked_by_act")
    pairs_ready, pairs_out, perm_in = sem("pairs_ready"), sem("pairs_out"), sem("perm_in")
    deg_ready, most_ready, plan_ready, places_ready = (sem("deg_ready"), sem("most_ready"), sem("plan_ready"),
                                                       sem("places_ready"))
    lo_ready, turned, moved, diag_ready = pair("lo_ready"), pair("turned"), pair("moved"), pair("diag_ready")
    matched, behind, finished = pair("matched"), pair("behind"), pair("finished")
    position_ready = sem("position_ready")
    blank_out = [sem(f"blank_out{q}") for q in range(2)]
    staged, placed = [sem(f"staged{r}") for r in range(RING)], [sem(f"placed{r}") for r in range(RING)]
    turns = sem("turns")

    def blanks(total):
        return (total + (BLANKS + 1)) // BLANKS

    def natural(ap, cols=1):
        return ap.rearrange("(b p) c -> p b c", p=P) if cols > 1 else ap.rearrange("(b p) c -> p (b c)", p=P)

    with nc.Block() as block:

        @block.sync
        def _(sp):
            for q in range(2):
                if q:
                    sp.wait_ge(key_read, 1)
                sp.dma_start(key_i[:, :], a["key_cols"][q]).then_inc(key_in, 16)
                sp.dma_start(pay[:, q, :, :], a["payloads"][q]).then_inc(pay_in, 16)
            sp.wait_ge(pay_in, 32)
            for q in range(2):
                def put(r, i):
                    at = bass.ds(i * (RING * H) + r * H, H)
                    sp.dma_start(stage_at[:, r, :], position[:, q, at]).then_inc(staged[r], 16)
                    sp.dma_start(stage_pay[:, r, :, :], pay[:, q, at, :]).then_inc(staged[r], 16)

                for k in range(CH):
                    sp.wait_ge(position_ready, q * CH + k + 1)
                    first = k * CR
                    if q == 0 and k == 0:
                        for r in range(RING):
                            put(r, 0)
                        first = 1
                    with sp.Fori(first, (k + 1) * CR) as i:
                        for r in range(RING):
                            sp.wait_ge(placed[r], i * (16 * H) + 16 * H * q * ROUNDS)
                            put(r, i)

        @block.gpsimd
        def _(pool):
            for q in range(2):
                pool.wait_ge(pairs_ready, q + 1)
                for b in range(NB):
                    pool.indirect_dma_start(c.perm_dram[q][:, :], bass.IndirectOffsetOnAxis(ap=rank_i[:, b:b + 1], axis=0),
                                            pairs[:, b, :], None).then_inc(pairs_out, 16)
                pool.wait_ge(deg_ready, q + 1)
                nc.gpsimd.partition_all_reduce(most[:, :], c.degs[q][:, :], P, RMAX).then_inc(most_ready, 1)
                pool.wait_ge(plan_ready, q + 1)
                total = pool.value_load(c.plans[q][0:1, 2 * NB:2 * NB + 1], min_val=NB, max_val=z.bodies)
                stand(pool, turns, blank_out[q], blanks(total) * 16)
                with pool.Fori(0, ROUNDS) as i:
                    for r in range(RING):
                        stand(pool, turns, staged[r], i * 32 + 32 * (q * ROUNDS + 1))
                        for j in range(H):
                            pool.indirect_dma_start(
                                c.ells[q][:, :], bass.IndirectOffsetOnAxis(ap=stage_at[:, r, j:j + 1], axis=0),
                                stage_pay[:, r, j, :], None).then_inc(placed[r], 16)
            for r in range(RING):
                pool.wait_ge(placed[r], 16 * H * 2 * ROUNDS)

        @block.tensor
        def _(pe):
            for q in range(2):
                with pe.Fori(0, ST) as i:
                    for h in range(HALVES):
                        pe.wait_ge(hots_ready[h], i + (q * ST + 1))
                        pe.wait_ge(counts_kept[h], i + (q * ST + 1))
                        for j in range(H):
                            mm = pe.matmul(counts_ps[h][:, j, :], lo_hot[:, h, j, :], hi_hot[:, h, j, :],
                                           start=True, stop=True)
                        mm.then_inc(counts_ready[h], 1)
                pe.wait_ge(places_ready, q + 1)

                def turn(h, i, n):
                    pe.wait_ge(lo_ready[h], n + 1)
                    for j in range(H):
                        pe.transpose(turned_ps[h][:, j, :], lo_hot[:, h, j, :], ident_b[:, :])
                    pe.transpose(turned_ps[h][0:CK, H, :], code_at[:, h, :, :].rearrange("p j b -> p (j b)"),
                                 ident_b[:, :]).then_inc(turned[h], 1)

                def look(h, i, n):
                    pe.wait_ge(moved[h], n + 1)
                    pe.wait_ge(finished[h], n + 1)
                    for j in range(H):
                        pe.matmul(looked_ps[h][:, j, :, :].rearrange("p t n -> p (t n)"), loT[:, h, j, :],
                                  looked_in[:, h, j, :, :].rearrange("p t n -> p (t n)"), start=True, stop=True)
                    pe.wait_ge(diag_ready[h], n + 1)
                    pe.matmul(match_ps[h][:, :, :].rearrange("p j e -> p (j e)"), codeT[:, h, :],
                              diag[:, h, :, :].rearrange("p j e -> p (j e)"), start=True, stop=False)
                    pe.matmul(match_ps[h][:, :, :].rearrange("p j e -> p (j e)"), ident_b[:, :],
                              before[:, :, :].rearrange("p j e -> p (j e)"),
                              start=False, stop=True).then_inc(matched[h], 1)

                with pe.Fori(0, CH) as k:
                    at = k * CB
                    turn(0, at, at + q * ST)
                    turn(1, at, at + q * ST)
                    look(0, at, at + q * ST)
                    with pe.Fori(1, CB) as s:
                        i = at + s
                        turn(0, i, i + q * ST)
                        look(1, i + (-1), i + (q * ST - 1))
                        turn(1, i, i + q * ST)
                        look(0, i, i + q * ST)
                    look(1, at + (CB - 1), at + (q * ST + CB - 1))

        @block.scalar
        def _(act):
            for h in range(HALVES):
                act.sem_inc(counts_kept[h], 1)
            for q in range(2):
                with act.Fori(0, ST) as i:
                    for h in range(HALVES):
                        act.wait_ge(counts_ready[h], i + (q * ST + 1))
                        nc.scalar.copy(count[:, bass.ds(i * S + (h * H + 1), H), :],
                                       counts_ps[h][:, :, :]).then_inc(counts_kept[h], 1)
                act.wait_ge(order_ready, q + 1)
                act.dma_start(natural(c.order_dram), order[:, :], allow_slow_non_contiguous=True).then_inc(order_out, 16)
                act.dma_start(natural(c.degree_dram[q]), c.natural_deg[:, q, :],
                              allow_slow_non_contiguous=True).then_inc(order_out, 16)
                act.wait_ge(order_out, 32 * (q + 1))
                act.dma_start(order_row[:, :], c.order_dram.rearrange("n a -> a n")
                              .to_broadcast([P, z.rows])).then_inc(order_in, 16)
                act.wait_ge(order_in, 16 * (q + 1))
                for b in range(NV, NB):
                    last = nc.scalar.activation(above_a[:, :], order_row[:, :], ACT.Sign, bias=order_less[:, b:b + 1],
                                                accum_out=rank[:, b:b + 1])
                    last.then_inc(act_order, 1)
                    act.wait_ge(act_order, q * (NB - NV) + b - NV + 1)
                act.sem_inc(ranked_by_act, 1)
                act.wait_ge(pairs_out, 16 * NB * (q + 1))
                act.dma_start(c.perms[q][:, :, :], natural(c.perm_dram[q], 2)).then_inc(perm_in, 16)
                act.wait_ge(plan_ready, q + 1)
                total = act.value_load(c.plans[q][0:1, 2 * NB:2 * NB + 1], min_val=NB, max_val=z.bodies)
                with act.Fori(0, blanks(total)) as i:
                    act.dma_start(c.ells[q][bass.ds(i * (BLANKS * S * P), BLANKS * S * P), :]
                                  .rearrange("(p s) c -> p (s c)", p=P),
                                  blank[:, :, :].rearrange("p s c -> p (s c)")).then_inc(blank_out[q], 16)

                def move(h, i, n):
                    nc.scalar.copy(looked_in[:, h, :, 0, :], count[:, bass.ds(i * S + h * H, H), :])
                    act.wait_ge(turned[h], n + 1)
                    nc.scalar.copy(codeT[:, h, :], turned_ps[h][0:CK, H, :])
                    nc.scalar.copy(loT[:, h, :, :], turned_ps[h][:, 0:H, :]).then_inc(moved[h], 1)

                def tell(h, n):
                    act.wait_ge(matched[h], n + 2)
                    for j in range(H):
                        last = nc.scalar.activation(matched_at[:, h, j, :], match_ps[h][:, j, :], ACT.Relu,
                                                    accum_out=within[:, h, j:j + 1])
                    last.then_inc(behind[h], 1)

                with act.Fori(0, CH) as k:
                    at = k * CB + q * ST
                    for h in range(HALVES):
                        move(h, k * CB, at)
                    with act.Fori(1, CB) as s:
                        n = at + s
                        for h in range(HALVES):
                            tell(h, n + (-1))
                            move(h, k * CB + s, n)
                    for h in range(HALVES):
                        tell(h, at + (CB - 1))

        @block.vector
        def _(v):
            done = [0]

            def step(ins):
                done[0] += 1
                ins.then_inc(dve, 1)
                v.wait_ge(dve, done[0])

            V.memset(blank[:, :, 0:1], z.dummy)
            V.memset(blank[:, :, 1:2], 0)
            V.tensor_scalar(block_end[:, :], iota_row[0:CK, 0:H], float(BITS), None, ALU.mult)
            v.drain()
            V.tensor_scalar(block_mask[:, :], block_end[:, :], iota_col[0:CK, 0:1], None, ALU.is_le)
            V.tensor_scalar(block_end[:, :], block_end[:, :], float(BITS), None, ALU.add)
            v.drain()
            V.scalar_tensor_tensor(out=block_mask[:, :], in0=block_end[:, :], scalar=iota_col[0:CK, 0:1],
                                   in1=block_mask[:, :], op0=ALU.is_gt, op1=ALU.mult)
            V.tensor_scalar(node_f[:, :], iota_row[:, 0:NB], float(P), iota_col[:, 0:1], ALU.mult, ALU.add)
            for h in range(HALVES):
                v.sem_inc(finished[h], 1)
                v.sem_inc(matched[h], 1)

            for q in range(2):
                v.wait_ge(key_in, 16 * (q + 1))
                V.tensor_copy(key_f[:, :], key_i[:, :])
                V.tensor_scalar(part_i[:, :], key_i[:, :], P - 1, None, ALU.bitwise_and)
                v.drain()
                V.tensor_copy(lo_f[:, :], part_i[:, :])
                v.drain()
                V.tensor_tensor(hi_f[:, :], key_f[:, :], lo_f[:, :], ALU.subtract)
                for k in range(BITS):
                    v.drain()
                    V.tensor_scalar(part_i[:, :], key_i[:, :], k, 1, ALU.arith_shift_right, ALU.bitwise_and)
                    v.drain()
                    V.tensor_scalar(codes[:, :, k], part_i[:, :], 2.0, -1.0, ALU.mult, ALU.add)
                step(V.tensor_scalar(hi_f[:, :], hi_f[:, :], 1.0 / P, None, ALU.mult))
                v.sem_inc(key_read, 1)
                V.memset(count[:, 0, :], 0.0)

                def low(h, i):
                    return V.tensor_tensor(
                        lo_hot[:, h, :, :], spread(iota_rb[:, :], [P, H, P], 1),
                        spread(lo_f[:, bass.ds(i * S + h * H, H)], [P, H, P], 2), ALU.is_equal)

                def hots(h, i):
                    low(h, i)
                    V.tensor_tensor(
                        hi_hot[:, h, :, :], spread(iota_row[:, 0:NB], [P, H, NB], 1),
                        spread(hi_f[:, bass.ds(i * S + h * H, H)], [P, H, NB], 2),
                        ALU.is_equal).then_inc(hots_ready[h], 1)

                for h in range(HALVES):
                    hots(h, 0)
                with v.Fori(1, ST) as i:
                    for h in range(HALVES):
                        v.wait_ge(counts_ready[h], i + q * ST)
                        hots(h, i)
                for h in range(HALVES):
                    v.wait_ge(counts_kept[h], 1 + (q + 1) * ST)
                for b in range(NB):
                    V.tensor_tensor_scan(count[:, :, b], count[:, :, b], zero[:, 0:1].to_broadcast([P, TL + 1]), 0.0,
                                         ALU.add, ALU.add)
                v.drain()

                deg = c.natural_deg[:, q, :]
                step(V.tensor_copy(deg, count[:, TL, :]))
                step(V.tensor_scalar(order[:, :], deg, 4095.0, 4096.0, ALU.min, ALU.mult))
                step(V.tensor_tensor(order[:, :], order[:, :], node_f[:, :], ALU.subtract))
                V.tensor_scalar(order_less[:, :], order[:, :], -1.0, None, ALU.mult).then_inc(order_ready, 1)
                V.tensor_copy(pairs[:, :, 0], node_f[:, :])
                V.tensor_copy(pairs[:, :, 1], deg)
                v.wait_ge(order_in, 16 * (q + 1))
                for b in range(NV):
                    step(V.tensor_scalar(above_v[:, :], order_row[:, :], order[:, b:b + 1], None, ALU.is_gt, ALU.add,
                                         accum_out=rank[:, b:b + 1]))
                v.wait_ge(ranked_by_act, q + 1)
                step(V.tensor_scalar(rank[:, NV:NB], rank[:, NV:NB], 0.5, 0.5 * (z.rows - 1), ALU.mult, ALU.add))
                step(V.tensor_copy(rank_i[:, :], rank[:, :]))
                v.sem_inc(pairs_ready, 1)
                step(V.tensor_scalar(rank_lo_i[:, :], rank_i[:, :], P - 1, None, ALU.bitwise_and))
                step(V.tensor_copy(rank_lo[:, :], rank_lo_i[:, :]))
                step(V.tensor_tensor(rank_hi[:, :], rank[:, :], rank_lo[:, :], ALU.subtract))
                step(V.tensor_scalar(rank_hi[:, :], rank_hi[:, :], 1.0 / P, None, ALU.mult))
                step(V.tensor_tensor(block_hot[:, :, :], spread(iota_row[:, 0:NB], [P, NB, NB], 1),
                                     spread(rank_hi[:, :], [P, NB, NB], 2), ALU.is_equal))

                v.wait_ge(perm_in, 16 * (q + 1))
                V.tensor_copy(c.degs[q][:, :], c.perms[q][:, :, 1]).then_inc(deg_ready, 1)
                v.wait_ge(most_ready, q + 1)
                step(V.tensor_scalar(nb_i[:, :], most[:, :], 1.0, float(H - 1), ALU.max, ALU.add))
                step(V.tensor_scalar(halves_i[:, :], nb_i[:, :], 2, None, ALU.arith_shift_right))
                step(V.tensor_scalar(nb_i[:, :], halves_i[:, :], 1, None, ALU.arith_shift_right))
                step(V.tensor_copy(full_f[:, :], nb_i[:, :]))
                step(V.tensor_copy(nb_f[:, :], halves_i[:, :]))
                step(V.tensor_scalar(nb_i[:, :], nb_f[:, :], 1.0, None, ALU.add))
                step(V.tensor_scalar(nb_i[:, :], nb_i[:, :], 1, None, ALU.arith_shift_right))
                step(V.tensor_copy(nb_f[:, :], nb_i[:, :]))
                step(V.tensor_tensor_scan(end_f[:, :], nb_f[:, :], zero[:, 0:1].to_broadcast([P, NB]), 0.0,
                                          ALU.add, ALU.add))
                step(V.tensor_tensor(base_f[:, :], end_f[:, :], nb_f[:, :], ALU.subtract))
                step(V.tensor_tensor_scan(second_f[:, :], full_f[:, :], zero[:, 0:1].to_broadcast([P, NB]), 0.0,
                                          ALU.add, ALU.add))
                step(V.tensor_tensor(full_f[:, :], second_f[:, :], full_f[:, :], ALU.subtract))
                V.tensor_copy(c.plans[q][:, NB:2 * NB], full_f[:, :])
                V.tensor_copy(c.plans[q][:, 2 * NB:2 * NB + 1], end_f[:, NB - 1:NB])
                V.tensor_copy(c.plans[q][:, 2 * NB + 1:2 * NB + 2], second_f[:, NB - 1:NB])
                step(V.tensor_copy(nb_i[:, :], base_f[:, :]))
                step(V.tensor_scalar(nb_i[:, :], nb_i[:, :], HALF_BITS, None, ALU.logical_shift_left))
                step(V.tensor_tensor(c.plans[q][:, 0:NB], nb_i[:, :], halves_i[:, :], ALU.bitwise_or))
                v.sem_inc(plan_ready, 1)
                step(V.tensor_tensor(block_hot[:, :, :], block_hot[:, :, :], spread(base_f[:, :], [P, NB, NB], 1),
                                     ALU.mult))
                step(V.tensor_reduce(place[:, :], block_hot[:, :, :], AX.X, ALU.add))
                step(V.scalar_tensor_tensor(out=place[:, :], in0=place[:, :], scalar=float(P), in1=rank_lo[:, :],
                                            op0=ALU.mult, op1=ALU.add))
                step(V.tensor_scalar(place[:, :], place[:, :], float(S), None, ALU.mult))
                for h in range(HALVES):
                    last = V.tensor_copy(looked_in[:, h, :, 1, :], spread(place[:, :], [P, H, NB], 1))
                step(last)
                v.sem_inc(places_ready, 1)

                def lows(h, i):
                    V.tensor_copy(code_at[:, h, :, :], codes[:, bass.ds(i * S + h * H, H), :])
                    low(h, i).then_inc(lo_ready[h], 1)

                def diagonal(h, n):
                    v.wait_ge(moved[h], n + 1)
                    v.wait_ge(matched[h], n + 1)
                    V.tensor_tensor(diag[:, h, :, :], spread(codeT[:, h, :], [CK, H, P], 1),
                                    spread(block_mask[:, :], [CK, H, P], 2), ALU.mult).then_inc(diag_ready[h], 1)

                def finish(h, i, n):
                    at = bass.ds(i * S + h * H, H)
                    V.tensor_tensor(hi_sel[:, h, :, :], spread(iota_row[:, 0:NB], [P, H, NB], 1),
                                    spread(hi_f[:, at], [P, H, NB], 2), ALU.is_equal)
                    v.drain()
                    v.wait_ge(behind[h], n + 1)
                    V.tensor_tensor(picked[:, h, :, :, :], looked_ps[h][:, :, :, :],
                                    spread(hi_sel[:, h, :, :], [P, H, 2, NB], 2), ALU.mult)
                    V.tensor_copy(ahead[:, at], within[:, h, :])
                    v.drain()
                    v.sem_inc(finished[h], 1)
                    V.tensor_reduce(found[:, at, :], picked[:, h, :, :, :], AX.X, ALU.add)

                with v.Fori(0, CH) as k:
                    at = k * CB
                    lows(0, at)
                    lows(1, at)
                    diagonal(0, at + q * ST)
                    with v.Fori(1, CB) as s:
                        i = at + s
                        lows(0, i)
                        diagonal(1, i + (q * ST - 1))
                        finish(0, i + (-1), i + (q * ST - 1))
                        lows(1, i)
                        diagonal(0, i + q * ST)
                        finish(1, i + (-1), i + (q * ST - 1))
                    diagonal(1, at + (q * ST + CB - 1))
                    for h in range(HALVES):
                        finish(h, at + (CB - 1), at + (q * ST + CB - 1))
                    v.drain()
                    part = bass.ds(k * (CB * S), CB * S)
                    V.tensor_tensor(ahead[:, part], ahead[:, part], found[:, part, 0], ALU.add)
                    v.drain()
                    V.tensor_copy(eighth_i[:, :], ahead[:, part])
                    v.drain()
                    V.tensor_scalar(eighth_i[:, :], eighth_i[:, :], 3, None, ALU.arith_shift_right)
                    v.drain()
                    V.tensor_copy(eighth[:, :], eighth_i[:, :])
                    v.drain()
                    V.scalar_tensor_tensor(out=ahead[:, part], in0=eighth[:, :], scalar=float(S * P - S),
                                           in1=ahead[:, part], op0=ALU.mult, op1=ALU.add)
                    v.drain()
                    V.tensor_tensor(position[:, q, part], ahead[:, part], found[:, part, 1], ALU.add)
                    v.drain()
                    v.sem_inc(position_ready, 1)


class Semaphores:

    def __init__(self, nc):
        self.nc, self.held = nc, []

    def __enter__(self):
        return self

    def sem(self, name):
        self.held.append(self.nc.alloc_semaphore(name=name))
        return self.held[-1]

    def __exit__(self, *failure):
        if failure[0] is None:
            self.nc.all_engine_barrier()
            self.nc.clear_and_free_semaphores(self.held)
            self.nc.all_engine_barrier()


class Projection:

    def __init__(self, nc, ctx, top, z, name, chunks, width):
        self.nc, self.z, self.chunks, self.width = nc, z, chunks, width
        self.group = 5
        self.groups = z.blocks // self.group
        assert self.groups * self.group == z.blocks
        per_bank = 512 // width
        room = -(-self.group // per_bank) * per_bank
        turned = -(-self.group * chunks // 4) * 4
        self.turned_ps = ctx.enter_context(nc.psum_tensor(f"{name}_turned_ps", [P, turned, P], F32))
        self.product_ps = ctx.enter_context(nc.psum_tensor(f"{name}_product_ps", [P, room, width], F32))
        self.turned_sb = ctx.enter_context(nc.sbuf_tensor(f"{name}_turned_sb", [P, self.group * chunks, P], F32))
        self.source_ready = top.sem(f"{name}_source_ready")
        self.turned = top.sem(f"{name}_turned")
        self.moved = top.sem(f"{name}_moved")
        self.projected = top.sem(f"{name}_projected")
        self.taken = top.sem(f"{name}_taken")

    def open(self, v):
        v.sem_inc(self.taken, 1)

    def tensor(self, pe, use, source, weights, ident):
        pe.wait_ge(self.source_ready, use + 1)
        for g in range(self.groups):
            n = use * self.groups + (g + 1)
            for k in range(self.group):
                for c in range(self.chunks):
                    mm = pe.transpose(self.turned_ps[:, k * self.chunks + c, :],
                                      source(g * self.group + k, c), ident)
            mm.then_inc(self.turned, 1)
            pe.wait_ge(self.moved, n)
            pe.wait_ge(self.taken, n)
            for k in range(self.group):
                for c in range(self.chunks):
                    mm = pe.matmul(self.product_ps[:, k, :], self.turned_sb[:, k * self.chunks + c, :],
                                   weights(c), start=(c == 0), stop=(c == self.chunks - 1))
            mm.then_inc(self.projected, 1)

    def scalar(self, act, use):
        with act.Fori(0, self.groups) as g:
            act.wait_ge(self.turned, use * self.groups + g + 1)
            self.nc.scalar.copy(self.turned_sb[:, :, :],
                                self.turned_ps[:, 0:self.group * self.chunks, :]).then_inc(self.moved, 1)

    def vector(self, v, use, take):
        with v.Fori(0, self.groups) as g:
            v.wait_ge(self.projected, use * self.groups + g + 1)
            take(g * self.group, self.product_ps[:, 0:self.group, :]).then_inc(self.taken, 1)
        v.drain()


def spread(ap, shape, axis):
    return ap.unsqueeze(axis).to_broadcast(shape)


def normalize(nc, top, z, name, x, h, work, col):
    NB = z.blocks
    order = top.sem(f"{name}_order")
    spread_ready = top.sem(f"{name}_spread_ready")
    root_ready = top.sem(f"{name}_root_ready")
    with nc.Block() as block:
        @block.vector
        def _(v):
            wide = [P, NB, D]
            nc.vector.tensor_reduce(col[:, 0, :], x[:, :, :], AX.X, ALU.add)
            v.drain()
            nc.vector.tensor_scalar(col[:, 0, :], col[:, 0, :], 1.0 / D, None, ALU.mult)
            v.drain()
            nc.vector.tensor_tensor(h[:, :, :], x[:, :, :], spread(col[:, 0, :], wide, 2), ALU.subtract)
            v.drain()
            nc.vector.tensor_tensor(work[:, :, :], h[:, :, :], h[:, :, :], ALU.mult)
            v.drain()
            nc.vector.tensor_reduce(col[:, 1, :], work[:, :, :], AX.X, ALU.add)
            v.drain()
            nc.vector.tensor_scalar(col[:, 1, :], col[:, 1, :], 1.0 / D, 1e-5, ALU.mult,
                                    ALU.add).then_inc(spread_ready, 1)
            v.wait_ge(root_ready, 1)
            nc.vector.reciprocal(col[:, 3, :], col[:, 2, :])
            v.drain()
            nc.vector.tensor_tensor(h[:, :, :], h[:, :, :], spread(col[:, 3, :], wide, 2), ALU.mult)
            v.drain()
            nc.vector.tensor_scalar(h[:, :, :], h[:, :, :], 0.0, None, ALU.max).then_inc(order, 1)
            v.wait_ge(order, 1)

        @block.scalar
        def _(act):
            act.wait_ge(spread_ready, 1)
            nc.scalar.activation(col[:, 2, :], col[:, 1, :], ACT.Sqrt).then_inc(root_ready, 1)


def scatter_rows(pool, z, perm, table, rows, sem, blocks=None):
    for b in blocks or range(z.blocks):
        pool.indirect_dma_start(table[:, :], bass.IndirectOffsetOnAxis(ap=perm[:, b, 0:1], axis=0),
                                rows[:, b, :], None).then_inc(sem, 16)


def gather_rows(pool, z, perm, table, rows, sem):
    for b in range(z.blocks):
        pool.indirect_dma_start(rows[:, b, :], None, table[:, :],
                                bass.IndirectOffsetOnAxis(ap=perm[:, b, 0:1], axis=0)).then_inc(sem, 16)


class Stream:

    def __init__(self, nc, ctx, top, z, name, ell, plan, width, sources=1):
        self.nc, self.z, self.ell, self.plan = nc, z, ell, plan
        self.per_half = 16 * H * sources
        self.index = ctx.enter_context(nc.sbuf_tensor(f"{name}_index", [P, HALVES, H, 2], I32))
        self.land = ctx.enter_context(nc.sbuf_tensor(f"{name}_land", [P, S, width], F32))

        def sem(what):
            return top.sem(f"{name}_{what}")

        self.index_in = [sem(f"index_in{h}") for h in range(HALVES)]
        self.landed = [sem(f"landed{h}") for h in range(HALVES)]
        self.land_free = [sem(f"land_free{h}") for h in range(HALVES)]
        self.table_in = sem("table_in")
        self.turns, self.index_turns = sem("turns"), sem("index_turns")

    def total(self, eng):
        NB = self.z.blocks
        return eng.value_load(self.plan[0:1, 2 * NB:2 * NB + 1], min_val=NB, max_val=self.z.bodies)

    def block(self, eng, b):
        most = self.z.bodies
        word = eng.value_load(self.plan[0:1, bass.ds(b, 1)], min_val=1, max_val=(1 << 31) - 1)
        halves = word & ((1 << HALF_BITS) - 1)
        return (eng.snap(((halves + 1) >> 1).with_bounds(min_val=1, max_val=most)),
                eng.snap((halves >> 1).with_bounds(min_val=0, max_val=most)),
                eng.snap((word >> HALF_BITS).with_bounds(min_val=0, max_val=most)))

    def second(self, eng, b):
        NB = self.z.blocks
        return eng.value_load(self.plan[0:1, bass.ds(b + NB, 1)], min_val=0, max_val=self.z.bodies)

    def all_second(self, eng):
        NB = self.z.blocks
        return eng.value_load(self.plan[0:1, 2 * NB + 1:2 * NB + 2], min_val=0, max_val=self.z.bodies)

    def by_halves(self, eng, bodies, seconds, visit, finish=lambda n: None):
        with eng.Fori(0, self.z.blocks) as b:
            many, whole, first = self.block(eng, b)
            n0 = eng.snap(bodies + first)
            n1 = eng.snap(seconds + self.second(eng, b))
            with eng.Fori(0, many) as i:
                visit(n0 + i, 0, first + i)
                with eng.If(i < whole):
                    visit(n1 + i, 1, first + i)
                finish(n0 + i)

    def open(self, pool, table, lands):
        for h in range(HALVES):
            for j in range(H):
                for land in lands:
                    pool.dma_start(land[:, h * H + j, :],
                                   table[self.z.rows:self.z.rows + P, :]).then_inc(self.landed[h], 16)
        for h in range(HALVES):
            pool.wait_ge(self.landed[h], self.per_half)

    def wait(self, eng, n, h):
        eng.wait_ge(self.landed[h], n * self.per_half + 2 * self.per_half)

    def rows(self, body):
        return self.ell[bass.ds(body * (S * P), S * P), :].rearrange("(p s) c -> p s c", p=P)

    def part(self, body, h):
        return self.rows(body)[:, h * H:(h + 1) * H, :]

    def load(self, sp, n, body, h, first=False):
        if not first:
            sp.wait_ge(self.landed[h], n * self.per_half)
        sp.dma_start(self.index[:, h, :, :], self.part(body, h)).then_inc(self.index_in[h], 16)

    def load(self, sp, n, h, body):
        sp.wait_ge(self.landed[h], n * self.per_half + self.per_half)
        sp.dma_start(self.index[:, h, :, :], self.part(body, h)).then_inc(self.index_in[h], 16)

    def load_all(self, sp, bodies, seconds):
        def visit(n, h, body):
            self.load(sp, n, h, body.with_bounds(min_val=0, max_val=self.z.bodies - 1))

        self.by_halves(sp, bodies, seconds, visit)

    def gather_all(self, pool, bodies, seconds, sources):
        self.by_halves(pool, bodies, seconds, lambda n, h, body: self.gather(pool, n, h, sources))

    def gather(self, pool, n, h, sources):
        stand(pool, self.turns, self.index_in[h], n * 16 + 16)
        stand(pool, self.turns, self.land_free[h], n + 1)
        for j in range(H):
            for table, c, land in sources:
                pool.indirect_dma_start(
                    land[:, h * H + j, :], None, table[:, :],
                    bass.IndirectOffsetOnAxis(ap=self.index[:, h, j, c:c + 1], axis=0)).then_inc(self.landed[h], 16)


class Softmax:

    def __init__(self, nc, ctx, top, name, heads):
        self.nc, self.heads = nc, heads

        def sb(what, shape):
            return ctx.enter_context(nc.sbuf_tensor(f"{name}_{what}", shape, F32))

        self.score = sb("score", [P, S, heads])
        self.absent = sb("absent", [P, S])
        self.left = sb("left_over", [P, 1])
        self.top_now = sb("top_now", [P, heads])
        self.top_body = sb("top_body", [P, heads])
        self.top_new = sb("top_new", [P, heads])
        self.drop = sb("drop", [P, heads])
        self.prob = sb("prob", [P, S, heads])
        self.keep = sb("keep", [P, heads])
        self.part = sb("prob_sum", [P, heads])
        self.denom = sb("denom", [P, heads])
        self.score_ready = top.sem(f"{name}_score_ready")
        self.prob_ready = top.sem(f"{name}_prob_ready")

    def begin(self, degree):
        self.clear()
        self.nc.vector.tensor_copy(self.left[:, :], degree)

    def clear(self):
        self.nc.vector.memset(self.top_now[:, :], NEG)
        self.nc.vector.memset(self.denom[:, :], 0.0)

    def mark(self, iota_row):
        self.nc.vector.tensor_scalar(self.absent[:, :], iota_row[:, 0:S], self.left[:, 0:1], ABSENT,
                                     ALU.is_ge, ALU.mult)

    def scores(self, v):
        V, n = self.nc.vector, self.heads
        V.tensor_scalar(self.left[:, :], self.left[:, :], float(-S), None, ALU.add)
        V.tensor_tensor(self.score[:, :, :], self.score[:, :, :], spread(self.absent[:, :], [P, S, n], 2), ALU.add)
        v.drain()
        V.tensor_reduce(self.top_body[:, :], self.score[:, :, :].rearrange("p s h -> p h s"), AX.X, ALU.max)
        v.drain()
        V.tensor_tensor(self.top_new[:, :], self.top_now[:, :], self.top_body[:, :], ALU.max)
        v.drain()
        V.tensor_tensor(self.drop[:, :], self.top_now[:, :], self.top_new[:, :], ALU.subtract)
        V.tensor_tensor(self.score[:, :, :], self.score[:, :, :], spread(self.top_new[:, :], [P, S, n], 1),
                        ALU.subtract).then_inc(self.score_ready, 1)

    def exponentials(self, act, n):
        act.wait_ge(self.score_ready, n + 1)
        self.nc.scalar.activation(self.keep[:, :], self.drop[:, :], ACT.Exp)
        self.nc.scalar.activation(self.prob[:, :, :], self.score[:, :, :], ACT.Exp).then_inc(self.prob_ready, 1)

    def weigh(self, v, n, values, weighed, total, part, width):
        h = self.heads
        v.wait_ge(self.prob_ready, n + 1)
        self.nc.vector.tensor_tensor(weighed[:, :, :].rearrange("p s (h c) -> p s h c", h=h),
                                     values.rearrange("p s (h c) -> p s h c", h=h),
                                     spread(self.prob[:, :, :], [P, S, h, width // h], 3), ALU.mult)
        self.add(v, weighed, total, part, width)

    def add(self, v, weighed, total, part, width):
        V, h = self.nc.vector, self.heads
        V.tensor_copy(self.top_now[:, :], self.top_new[:, :])
        V.tensor_reduce(self.part[:, :], self.prob[:, :, :].rearrange("p s h -> p h s"), AX.X, ALU.add)
        V.tensor_tensor(self.denom[:, :], self.denom[:, :], self.keep[:, :], ALU.mult)
        V.tensor_tensor(total[:, :].rearrange("p (h c) -> p h c", h=h), total[:, :].rearrange("p (h c) -> p h c", h=h),
                        spread(self.keep[:, :], [P, h, width // h], 2), ALU.mult)
        v.drain()
        V.tensor_reduce(part[:, :], weighed[:, :, :].rearrange("p s f -> p f s"), AX.X, ALU.add)
        V.tensor_tensor(self.denom[:, :], self.denom[:, :], self.part[:, :], ALU.add)
        v.drain()
        V.tensor_tensor(total[:, :], total[:, :], part[:, :], ALU.add)


def attention_over_relations(nc, top, z, c, a, x, h, res, work):
    NB, HOPS, KINDS = z.blocks, 3, 64
    with ExitStack() as ctx:
        def sb(name, shape, dt=F32):
            return ctx.enter_context(nc.sbuf_tensor(name, shape, dt))

        def sem(name):
            return top.sem(name)

        q_w, k_w = sb("q_w", [P, D]), sb("k_w", [P, D])
        relation = sb("relation", [P, D])
        rest = sb("rest", [P, D])
        parts = sb("relation_parts", [P, 3, 2, D], BF16)
        left, left_now = sb("left", [P, NB, D]), sb("left_now", [P, D])
        kind = sb("kind", [P, S, 2], I32)
        hot = sb("hot", [P, S, KINDS], BF16)
        hotT = sb("hotT", [P, S // 2, P], BF16)
        message = sb("message", [P, S, D])
        kept = sb("kept", [P, 2, S, D])
        messageT = sb("messageT", [P, HALVES, H, P])
        right = sb("right", [P, S, D])
        product = sb("product", [P, S, D])
        weighed = sb("weighed", [P, S, D])
        total, part = sb("total", [P, D]), sb("part", [P, D])
        scale = sb("scale", [P, 1])
        share = sb("share", [P, NB])
        col = sb("norm_col", [P, 4, NB])
        stream = Stream(nc, ctx, top, z, "l0", c.ells[0], c.plans[0], D)
        soft = Softmax(nc, ctx, top, "l0", 1)
        kind_in, kind_free, hot_ready = sem("kind_in"), sem("kind_free"), sem("hot_ready")
        hotT_ready, hotT_moved = sem("hotT_ready"), sem("hotT_moved")
        rel_ready = [sem(f"rel_ready{k}") for k in range(HALVES)]
        message_ready = [sem(f"message_ready{k}") for k in range(HALVES)]
        messageT_ready = [sem(f"messageT_ready{k}") for k in range(HALVES)]
        messageT_moved = [sem(f"messageT_moved{k}") for k in range(HALVES)]
        right_ready = [sem(f"right_ready{k}") for k in range(HALVES)]
        right_out = [sem(f"right_out{k}") for k in range(HALVES)]
        right_used = [sem(f"right_used{k}") for k in range(HALVES)]
        kept_ready = [sem(f"kept_ready{k}") for k in range(HALVES)]
        weights_in = sem("l0_weights_in")
        weighed_ready = [sem(f"weighed_ready{k}") for k in range(HALVES)]
        sums_ready = sem("l0_sums_ready")
        norms_ready = sem("l0_norms_ready")
        proj = Projection(nc, ctx, top, z, "left", 1, D)
        hotT_ps = ctx.enter_context(nc.psum_tensor("hotT_ps", [P, S, P], BF16))
        messageT_ps = proj.turned_ps
        right_ps = proj.product_ps
        rel_ps = ctx.enter_context(nc.psum_tensor("rel_ps", [P, S, P], F32))

        with nc.Block() as block:

            @block.sync
            def _(sp):
                sp.dma_start(q_w[:, :], a["q_w"]).then_inc(weights_in, 16)
                sp.dma_start(k_w[:, :], a["k_w"]).then_inc(weights_in, 16)
                for k in range(2):
                    sp.dma_start(relation[k * KINDS:(k + 1) * KINDS, :], a["edge_emb"]).then_inc(weights_in, 16)
                sp.sem_inc(kind_free, 1)
                all_bodies = stream.total(sp)
                with sp.Fori(0, HOPS) as hop:
                    sp.wait_ge(proj.source_ready, hop + 1)

                    def kinds(body):
                        sp.wait_ge(kind_free, hop * (all_bodies + 2) + body + 1)
                        sp.dma_start(kind[:, :, :], stream.rows(body)).then_inc(kind_in, 16)

                    kinds(0)
                    for k in range(HALVES):
                        stream.load(sp, hop * (all_bodies + 1), k, 0)
                    with sp.Fori(1, all_bodies + 1) as body:
                        kinds(body)
                        for k in range(HALVES):
                            stream.load(sp, hop * (all_bodies + 1) + body, k, body)
                    kinds(all_bodies + 1)

            @block.gpsimd
            def _(pool):
                stream.open(pool, c.table, [stream.land])
                all_bodies = stream.total(pool)
                with pool.Fori(0, HOPS) as hop:
                    pool.wait_ge(proj.source_ready, hop + 1)
                    pool.sem_inc(stream.turns, 1)
                    scatter_rows(pool, z, c.perms[0], c.table, res, stream.table_in)
                    stand(pool, stream.turns, stream.table_in, hop * z.stored + z.stored)
                    with pool.Fori(0, all_bodies + 1) as body:
                        for k in range(HALVES):
                            stream.gather(pool, hop * (all_bodies + 1) + body, k, [(c.table, 0, stream.land)])

            @block.tensor
            def _(pe):
                all_bodies = stream.total(pe)
                pe.wait_ge(weights_in, 64)

                def turn_kinds(m):
                    pe.wait_ge(hot_ready, m + 1)
                    for j in range(S // 2):
                        mm = pe.transpose(hotT_ps[:, j, :], hot[:, 2 * j:2 * j + 2, :].rearrange("p s n -> p (s n)"),
                                          c.ident_b[:, :])
                    mm.then_inc(hotT_ready, 1)

                def relations(m, k):
                    pe.wait_ge(hotT_moved, m + 2)
                    for j in range(H // 2):
                        pair = slice(k * H + 2 * j, k * H + 2 * j + 2)
                        for t in range(3):
                            mm = pe.matmul(rel_ps[:, pair, :].rearrange("p s d -> p (s d)"), hotT[:, k * (H // 2) + j, :],
                                           parts[:, t, :, :].rearrange("p s d -> p (s d)"), start=(t == 0), stop=(t == 2))
                    mm.then_inc(rel_ready[k], 1)

                def rights(n, k):
                    pe.wait_ge(message_ready[k], n + 1)
                    for j in range(H):
                        mm = pe.transpose(messageT_ps[:, k * H + j, :], message[:, k * H + j, :], c.ident[:, :])
                    mm.then_inc(messageT_ready[k], 1)
                    pe.wait_ge(messageT_moved[k], n + 1)
                    pe.wait_ge(right_out[k], n + 1)
                    for j in range(H):
                        mm = pe.matmul(right_ps[:, k * H + j, :], messageT[:, k, j, :], k_w[:, :],
                                       start=True, stop=True)
                    mm.then_inc(right_ready[k], 1)

                with pe.Fori(0, HOPS) as hop:
                    n, m = pe.snap(hop * (all_bodies + 1)), pe.snap(hop * (all_bodies + 2))
                    proj.tensor(pe, hop, lambda b, _: res[:, b, :], lambda _: q_w[:, :], c.ident[:, :])
                    turn_kinds(m)
                    for k in range(HALVES):
                        relations(m, k)
                    turn_kinds(m + 1)
                    for k in range(HALVES):
                        rights(n, k)
                        relations(m + 1, k)
                    with pe.Fori(0, all_bodies) as i:
                        turn_kinds(m + i + 2)
                        for k in range(HALVES):
                            rights(n + i + 1, k)
                            relations(m + i + 2, k)

            @block.scalar
            def _(act):
                all_bodies = stream.total(act)
                for k in range(HALVES):
                    act.sem_inc(kept_ready[k], 1)
                    act.sem_inc(right_out[k], 1)
                act.sem_inc(hotT_moved, 1)

                def move_kinds(m):
                    act.wait_ge(hotT_ready, m + 1)
                    nc.scalar.copy(hotT[:, :, :], hotT_ps[:, 0:S // 2, :]).then_inc(hotT_moved, 1)

                def move_messages(n, k):
                    half = slice(k * H, (k + 1) * H)
                    act.wait_ge(messageT_ready[k], n + 1)
                    nc.scalar.copy(messageT[:, k, :, :], messageT_ps[:, half, :]).then_inc(messageT_moved[k], 1)

                def keep(n, k):
                    half = slice(k * H, (k + 1) * H)
                    nc.scalar.copy(kept[:, bass.ds(n % 2, 1), half, :].rearrange("p a s d -> p (a s) d"),
                                   message[:, half, :]).then_inc(kept_ready[k], 1)

                def tanh(n, k):
                    half = slice(k * H, (k + 1) * H)
                    act.wait_ge(right_ready[k], n + 1)
                    act.wait_ge(right_used[k], n + 1)
                    nc.scalar.activation(right[:, half, :], right_ps[:, half, :], ACT.Tanh).then_inc(right_out[k], 1)

                def weigh(n, k):
                    for s in range(k * H, (k + 1) * H):
                        last = nc.scalar.activation(
                            weighed[:, s, :], kept[:, bass.ds(n % 2, 1), s, :].rearrange("p a d -> p (a d)"),
                            ACT.Copy, scale=soft.prob[:, s, :])
                    last.then_inc(weighed_ready[k], 1)

                with act.Fori(0, HOPS) as hop:
                    n, m = act.snap(hop * (all_bodies + 1)), act.snap(hop * (all_bodies + 2))
                    proj.scalar(act, hop)
                    move_kinds(m)
                    move_kinds(m + 1)
                    for k in range(HALVES):
                        move_messages(n, k)
                        keep(n, k)
                        tanh(n, k)
                    with act.Fori(0, all_bodies) as i:
                        move_kinds(m + i + 2)
                        move_messages(n + i + 1, 0)
                        keep(n + i + 1, 0)
                        tanh(n + i + 1, 0)
                        soft.exponentials(act, hop * all_bodies + i)
                        act.wait_ge(soft.prob_ready, hop * all_bodies + i + 1)
                        weigh(n + i, 0)
                        move_messages(n + i + 1, 1)
                        weigh(n + i, 1)
                        keep(n + i + 1, 1)
                        tanh(n + i + 1, 1)
                    act.wait_ge(sums_ready, hop + 1)
                    nc.scalar.activation(col[:, 1, :], col[:, 0, :], ACT.Sqrt).then_inc(norms_ready, 1)

            @block.vector
            def _(v):
                V = nc.vector
                all_bodies = stream.total(v)
                proj.open(v)
                for k in range(HALVES):
                    v.sem_inc(stream.land_free[k], 1)
                    v.sem_inc(right_used[k], 1)
                V.tensor_copy(res[:, :, :], h[:, :, :])
                v.wait_ge(weights_in, 64)
                V.memset(parts[:, :, :, :], 0.0)
                V.tensor_copy(rest[:, :], relation[:, :])
                v.drain()
                for t in range(3):
                    for k in range(2):
                        rows = slice(k * KINDS, (k + 1) * KINDS)
                        V.tensor_copy(parts[rows, t, k, :], rest[rows, :])
                    v.drain()
                    for k in range(2):
                        rows = slice(k * KINDS, (k + 1) * KINDS)
                        V.tensor_tensor(rest[rows, :], rest[rows, :], parts[rows, t, k, :], ALU.subtract)
                    v.drain()
                V.tensor_scalar(col[:, 0, :], c.degs[0][:, :], 1.0, None, ALU.max)
                V.tensor_scalar(col[:, 2, :], c.degs[0][:, :], 0.0, None, ALU.is_gt)
                v.drain()
                V.reciprocal(col[:, 1, :], col[:, 0, :])
                v.drain()
                V.tensor_tensor(share[:, :], col[:, 1, :], col[:, 2, :], ALU.mult)
                v.drain()
                v.sem_inc(proj.source_ready, 1)

                def kinds(m):
                    v.wait_ge(kind_in, m * 16 + 16)
                    v.wait_ge(hotT_moved, m + 1)
                    V.tensor_tensor(hot[:, :, :], spread(c.iota_row[:, 0:KINDS], [P, S, KINDS], 1),
                                    kind[:, :, 1:2].to_broadcast([P, S, KINDS]), ALU.is_equal).then_inc(hot_ready, 1)

                def free_kinds(m):
                    v.wait_ge(hot_ready, m + 1)
                    v.sem_inc(kind_free, 1)

                def messages(n, m, k):
                    half = slice(k * H, (k + 1) * H)
                    stream.wait(v, n, k)
                    v.wait_ge(rel_ready[k], m + 1)
                    v.wait_ge(kept_ready[k], n + 1)
                    V.tensor_tensor(message[:, half, :], stream.land[:, half, :], rel_ps[:, half, :],
                                    ALU.mult).then_inc(message_ready[k], 1)

                def add_body(n):
                    for k in range(HALVES):
                        v.wait_ge(weighed_ready[k], n)
                    soft.add(v, weighed, total, part, D)

                def finish_block(b):
                    v.drain()
                    V.tensor_scalar(soft.denom[:, :], soft.denom[:, :], 1.0, None, ALU.max)
                    v.drain()
                    V.reciprocal(scale[:, :], soft.denom[:, :])
                    v.drain()
                    V.tensor_tensor(scale[:, :], scale[:, :], share[:, bass.ds(b, 1)], ALU.mult)
                    v.drain()
                    V.tensor_scalar(res[:, bass.ds(b, 1), :].rearrange("p a d -> p (a d)"), total[:, :],
                                    scale[:, 0:1], None, ALU.mult)
                    v.drain()

                def free_rows(n, k):
                    v.wait_ge(message_ready[k], n + 1)
                    v.sem_inc(stream.land_free[k], 1)

                with v.Fori(0, HOPS) as hop:
                    def take(b, products):
                        return V.tensor_copy(left[:, bass.ds(b, proj.group), :], products)

                    proj.vector(v, hop, take)
                    v.wait_ge(stream.table_in, hop * z.stored + z.stored)
                    for j in range(2):
                        kinds(hop * (all_bodies + 2) + j)
                        free_kinds(hop * (all_bodies + 2) + j)
                    for k in range(HALVES):
                        messages(hop * (all_bodies + 1), hop * (all_bodies + 2), k)
                        free_rows(hop * (all_bodies + 1), k)
                    with v.Fori(0, NB) as b:
                        many, _, first = stream.block(v, b)
                        n0 = v.snap(hop * (all_bodies + 1) + first)
                        m0 = v.snap(hop * (all_bodies + 2) + first)
                        w0 = v.snap(hop * all_bodies + first)
                        V.tensor_copy(soft.left[:, :], c.degs[0][:, bass.ds(b, 1)])
                        V.tensor_copy(left_now[:, :], left[:, bass.ds(b, 1), :].rearrange("p a d -> p (a d)"))
                        v.drain()
                        with v.Fori(0, many) as i:
                            n = v.snap(n0 + i)
                            m = v.snap(m0 + i)
                            kinds(m + 2)
                            messages(n + 1, m + 1, 0)
                            soft.mark(c.iota_row)
                            free_kinds(m + 2)
                            free_rows(n + 1, 0)
                            with v.If(first + i > 0):
                                add_body(w0 + i)
                            with v.If(i < 1):
                                with v.If(b > 0):
                                    finish_block((b + (-1)).with_bounds(min_val=0, max_val=NB - 1))
                                soft.clear()
                                V.memset(total[:, :], 0.0)
                                v.drain()
                            for k in range(HALVES):
                                v.wait_ge(right_out[k], n + 2)
                                for s in range(k * H, (k + 1) * H):
                                    last = V.tensor_tensor_reduce(product[:, s, :], right[:, s, :], left_now[:, :],
                                                                  op0=ALU.mult, op1=ALU.add, scale=1.0, scalar=0.0,
                                                                  accum_out=soft.score[:, s, :])
                                last.then_inc(right_used[k], 1)
                            v.drain()
                            soft.scores(v)
                            messages(n + 1, m + 1, 1)
                            free_rows(n + 1, 1)
                    add_body(hop * all_bodies + all_bodies)
                    finish_block(NB - 1)
                    V.tensor_tensor(work[:, :, :], res[:, :, :], res[:, :, :], ALU.mult)
                    V.tensor_tensor(x[:, :, :], x[:, :, :], h[:, :, :], ALU.add)
                    v.drain()
                    V.tensor_reduce(col[:, 0, :], work[:, :, :], AX.X, ALU.add).then_inc(sums_ready, 1)
                    v.wait_ge(norms_ready, hop + 1)
                    V.tensor_scalar(col[:, 2, :], col[:, 1, :], 1e-12, None, ALU.max)
                    v.drain()
                    V.reciprocal(col[:, 3, :], col[:, 2, :])
                    v.drain()
                    V.tensor_tensor(res[:, :, :], res[:, :, :], spread(col[:, 3, :], [P, NB, D], 2), ALU.mult)
                    v.drain()
                    V.tensor_tensor(x[:, :, :], x[:, :, :], res[:, :, :], ALU.add)
                    v.drain()
                    for k in range(HALVES):
                        v.wait_ge(right_out[k], hop * (all_bodies + 1) + all_bodies + 2)
                        v.sem_inc(right_used[k], 1)
                    v.sem_inc(proj.source_ready, 1)


def graph_attention(nc, top, z, c, a, x, h, res, work):
    NB, LAYERS, HEADS = z.blocks, 3, 4
    C = D // HEADS
    W = D + HEADS
    with ExitStack() as ctx:
        def sb(name, shape, dt=F32):
            return ctx.enter_context(nc.sbuf_tensor(name, shape, dt))

        def sem(name):
            return top.sem(name)

        w = sb("gat_w", [P, LAYERS, 2, D])
        att = sb("gat_att", [P, LAYERS, 2, D])
        bias = sb("gat_bias", [P, LAYERS, D])
        floor = sb("gat_floor", [P, LAYERS])
        rows = sb("gat_rows", [P, NB, W])
        own = sb("gat_own", [P, NB, HEADS])
        scaled = sb("gat_scaled", [P, 5, 2, D])
        body_rows = sb("gat_body_rows", [P, 2, S, W])
        weighed = sb("gat_weighed", [P, S, D])
        raw = sb("gat_raw", [P, S, HEADS])
        total, part = sb("gat_total", [P, D]), sb("gat_part", [P, D])
        denom, inverse = sb("gat_denom", [P, HEADS]), sb("gat_inverse", [P, HEADS])
        stream = Stream(nc, ctx, top, z, "l1", c.ells[1], c.plans[1], W)
        soft = Softmax(nc, ctx, top, "l1", HEADS)
        proj = Projection(nc, ctx, top, z, "gat", 1, 2 * D)
        weights_in = sem("l1_weights_in")
        rows_ready = sem("l1_rows_ready")
        copied = [sem(f"l1_copied{k}") for k in range(HALVES)]
        rows_used, rows_turns = sem("l1_rows_used"), sem("l1_rows_turns")

        with nc.Block() as block:

            @block.sync
            def _(sp):
                for n in range(2):
                    sp.dma_start(w[:, :, n, :], a["gat_w"][n].rearrange("l k n -> k l n")).then_inc(weights_in, 16)
                    sp.dma_start(att[:, :, n, :], a["gat_att"][n].rearrange("(a l) n -> a l n", a=1)
                                 .to_broadcast([P, LAYERS, D])).then_inc(weights_in, 16)
                sp.dma_start(bias[:, :, :], a["gat_b"].rearrange("(a l) n -> a l n", a=1)
                             .to_broadcast([P, LAYERS, D])).then_inc(weights_in, 16)
                all_bodies, all_second = stream.total(sp), stream.all_second(sp)
                with sp.Fori(0, LAYERS) as layer:
                    stand(sp, stream.index_turns, rows_ready, layer * proj.groups + proj.groups)
                    stream.load_all(sp, layer * all_bodies, layer * all_second)

            @block.gpsimd
            def _(pool):
                stream.open(pool, c.table_w, [stream.land])
                all_bodies, all_second = stream.total(pool), stream.all_second(pool)
                with pool.Fori(0, LAYERS) as layer:
                    for g in range(proj.groups):
                        stand(pool, stream.turns, rows_ready, layer * proj.groups + g + 1)
                        scatter_rows(pool, z, c.perms[1], c.table_w, rows, stream.table_in,
                                     range(g * proj.group, (g + 1) * proj.group))
                    stand(pool, stream.turns, stream.table_in, layer * z.stored + z.stored)
                    stream.gather_all(pool, layer * all_bodies, layer * all_second, [(c.table_w, 0, stream.land)])

            @block.tensor
            def _(pe):
                pe.wait_ge(weights_in, 80)
                with pe.Fori(0, LAYERS) as layer:
                    proj.tensor(pe, layer, lambda b, _: res[:, b, :],
                                lambda _: w[:, bass.ds(layer, 1), :, :].rearrange("p a t d -> p (a t d)"),
                                c.ident[:, :])

            @block.scalar
            def _(act):
                all_bodies, all_second = stream.total(act), stream.all_second(act)

                def take_rows(n, h, body):
                    if h == 0:
                        act.wait_ge(rows_used, n + 1)
                    stream.wait(act, n, h)
                    nc.scalar.copy(body_rows[:, bass.ds(body % 2, 1), h * H:(h + 1) * H, :]
                                   .rearrange("p a s w -> p (a s) w"), stream.land[:, h * H:(h + 1) * H, :]).then_inc(copied[h], 1)
                    act.wait_ge(copied[h], n + 1)
                    act.sem_inc(stream.land_free[h], 1)

                with act.Fori(0, LAYERS) as layer:
                    proj.scalar(act, layer)
                    stream.by_halves(act, layer * all_bodies, layer * all_second, take_rows,
                                     lambda n: soft.exponentials(act, n))

            @block.vector
            def _(v):
                V = nc.vector
                all_bodies, all_second = stream.total(v), stream.all_second(v)
                proj.open(v)
                for k in range(HALVES):
                    v.sem_inc(stream.land_free[k], 1)
                V.memset(body_rows[:, :, :, :], 0.0)
                v.drain()
                v.sem_inc(rows_used, 1)
                v.sem_inc(rows_used, 1)
                V.memset(floor[:, 0:LAYERS - 1], 0.0)
                V.memset(floor[:, LAYERS - 1:LAYERS], -3.0e38)
                V.tensor_copy(res[:, :, :], h[:, :, :])
                v.wait_ge(weights_in, 80)
                v.drain()
                v.sem_inc(proj.source_ready, 1)
                with v.Fori(0, LAYERS) as layer:
                    def take(b, products):
                        at = bass.ds(b, proj.group)
                        both = products.rearrange("p g (t d) -> p g t d", t=2)
                        V.tensor_tensor(scaled[:, :, :, :].rearrange("p g t d -> p g (t d)"), products,
                                        att[:, bass.ds(layer, 1), :, :].rearrange("p a t d -> p a (t d)")
                                        .to_broadcast([P, proj.group, 2 * D]), ALU.mult)
                        last = V.tensor_copy(rows[:, at, 0:D], both[:, :, 0, :])
                        v.drain()
                        V.tensor_reduce(rows[:, at, D:W], scaled[:, :, 0, :].rearrange("p g (h c) -> p g h c", c=C),
                                        AX.X, ALU.add)
                        V.tensor_reduce(own[:, at, :], scaled[:, :, 1, :].rearrange("p g (h c) -> p g h c", c=C),
                                        AX.X, ALU.add)
                        v.drain()
                        v.sem_inc(rows_ready, 1)
                        return V.memset(part[:, 0:1], 0.0)

                    proj.vector(v, layer, take)
                    with v.Fori(0, NB) as b:
                        many, whole, first = stream.block(v, b)
                        soft.begin(c.degs[1][:, bass.ds(b, 1)])
                        V.memset(total[:, :], 0.0)
                        v.drain()
                        n0 = v.snap(layer * all_bodies + first)
                        n1 = v.snap(layer * all_second + stream.second(v, b))

                        with v.Fori(0, many) as i:
                            n = n0 + i
                            soft.mark(c.iota_row)
                            v.wait_ge(copied[0], n + 1)
                            with v.If(i < whole):
                                stand(v, rows_turns, copied[1], n1 + i + 1)
                            now = body_rows[:, bass.ds((first + i) % 2, 1), :, :].rearrange("p a s w -> p (a s) w")
                            V.tensor_tensor(raw[:, :, :], now[:, :, D:W],
                                            own[:, bass.ds(b, 1), :].to_broadcast([P, S, HEADS]), ALU.add)
                            v.drain()
                            V.scalar_tensor_tensor(out=soft.score[:, :, :], in0=raw[:, :, :], scalar=0.2,
                                                   in1=raw[:, :, :], op0=ALU.mult, op1=ALU.max)
                            v.drain()
                            soft.scores(v)
                            soft.weigh(v, n, now[:, :, 0:D], weighed, total, part, D)
                            v.drain()
                            v.sem_inc(rows_used, 1)
                        V.tensor_scalar(denom[:, :], soft.denom[:, :], 1e-16, None, ALU.add)
                        v.drain()
                        V.reciprocal(inverse[:, :], denom[:, :])
                        v.drain()
                        V.tensor_tensor(part[:, :].rearrange("p (h c) -> p h c", c=C),
                                        total[:, :].rearrange("p (h c) -> p h c", c=C),
                                        spread(inverse[:, :], [P, HEADS, C], 2), ALU.mult)
                        v.drain()
                        V.tensor_tensor(part[:, :], part[:, :],
                                        bias[:, bass.ds(layer, 1), :].rearrange("p a d -> p (a d)"), ALU.add)
                        v.drain()
                        V.tensor_scalar(res[:, bass.ds(b, 1), :].rearrange("p a d -> p (a d)"), part[:, :],
                                        floor[:, bass.ds(layer, 1)], None, ALU.max)
                        v.drain()
                    v.wait_ge(stream.table_in, layer * z.stored + z.stored)
                    v.sem_inc(proj.source_ready, 1)
                V.tensor_tensor(x[:, :, :], x[:, :, :], res[:, :, :], ALU.add)
                v.drain()


def sum_neighbours(nc, top, z, c, name, rows, res):
    NB = z.blocks
    with ExitStack() as ctx:
        total = ctx.enter_context(nc.sbuf_tensor(f"{name}_total", [P, D], F32))
        part = ctx.enter_context(nc.sbuf_tensor(f"{name}_part", [P, HALVES, D], F32))
        stream = Stream(nc, ctx, top, z, name, c.ells[1], c.plans[1], D)
        with nc.Block() as block:

            @block.sync
            def _(sp):
                stream.load_all(sp, 0, 0)

            @block.gpsimd
            def _(pool):
                stream.open(pool, c.table, [stream.land])
                scatter_rows(pool, z, c.perms[1], c.table, rows, stream.table_in)
                pool.wait_ge(stream.table_in, z.stored)
                stream.gather_all(pool, 0, 0, [(c.table, 0, stream.land)])

            @block.vector
            def _(v):
                V = nc.vector
                for k in range(HALVES):
                    v.sem_inc(stream.land_free[k], 1)
                v.wait_ge(stream.table_in, z.stored)

                def add(n, k):
                    stream.wait(v, n, k)
                    V.tensor_reduce(part[:, k, :], stream.land[:, k * H:(k + 1) * H, :]
                                    .rearrange("p s d -> p d s"), AX.X, ALU.add)
                    v.drain()
                    v.sem_inc(stream.land_free[k], 1)
                    V.tensor_tensor(total[:, :], total[:, :], part[:, k, :], ALU.add)
                    v.drain()

                with v.Fori(0, NB) as b:
                    many, whole, first = stream.block(v, b)
                    second = stream.second(v, b)
                    V.memset(total[:, :], 0.0)
                    v.drain()
                    with v.Fori(0, many) as i:
                        add(first + i, 0)
                        with v.If(i < whole):
                            add(second + i, 1)
                    V.tensor_copy(res[:, bass.ds(b, 1), :].rearrange("p a d -> p (a d)"), total[:, :])
                    v.drain()


def project(nc, top, z, c, name, chunks, width, weights_in, count, source, weights, target, finish):
    with ExitStack() as ctx:
        proj = Projection(nc, ctx, top, z, name, chunks, width)
        with nc.Block() as block:

            @block.tensor
            def _(pe):
                pe.wait_ge(weights_in, count)
                pe.sem_inc(proj.source_ready, 1)
                proj.tensor(pe, 0, source, weights, c.ident[:, :])

            @block.scalar
            def _(act):
                proj.scalar(act, 0)

            @block.vector
            def _(v):
                proj.open(v)
                v.wait_ge(weights_in, count)

                def take(b, products):
                    return nc.vector.tensor_copy(target[:, bass.ds(b, proj.group), :], products)

                proj.vector(v, 0, take)
                finish(v)


def graph_convolution(nc, top, z, c, a, x, h, res, work):
    NB = z.blocks
    WIDE = 2 * D
    with ExitStack() as ctx:
        def sb(name, shape, dt=F32):
            return ctx.enter_context(nc.sbuf_tensor(name, shape, dt))

        def sem(name):
            return top.sem(name)

        w1, w2 = sb("w1", [P, WIDE]), sb("w2", [P, 2, D])
        fc1, fc2 = sb("fc1", [P, D]), sb("fc2", [P, D])
        b1, b2, fb1, fb2 = sb("b1", [P, WIDE]), sb("b2", [P, D]), sb("fb1", [P, D]), sb("fb2", [P, D])
        norm_src, norm_dst = sb("norm_src", [P, NB]), sb("norm_dst", [P, NB])
        out_degree = sb("out_degree", [P, NB])
        degree_in = sem("l2_degree_in")
        col = sb("gcn_col", [P, 4, NB])
        hidden = sb("hidden", [P, NB, WIDE])
        weights_in = sem("l2_weights_in")
        counts_ready, roots_ready = sem("l2_counts_ready"), sem("l2_roots_ready")
        exp_in, exp_out = sem("l2_exp_in"), sem("l2_exp_out")
        loads = [(w1[:, :], a["w1"]), (w2[:, :, :], a["w2"].rearrange("(c k) n -> k c n", k=P)), (fc1[:, :], a["fc1"]),
                 (fc2[:, :], a["fc2"])]
        loads += [(to[:, :], a[k].rearrange("(a n) -> a n", a=1).to_broadcast([P, to.shape[1]]))
                  for to, k in ((b1, "b1"), (b2, "b2"), (fb1, "fb1"), (fb2, "fb2"))]
        arrived = 16 * len(loads)

        with nc.Block() as block:
            @block.sync
            def _(sp):
                for to, of in loads:
                    sp.dma_start(to, of).then_inc(weights_in, 16)

            @block.gpsimd
            def _(pool):
                gather_rows(pool, z, c.perms[1], c.degree_dram[0], out_degree[:, :].unsqueeze(2), degree_in)

            @block.vector
            def _(v):
                V = nc.vector
                v.wait_ge(degree_in, z.stored)
                V.tensor_scalar(col[:, 0, :], out_degree[:, :], 1.0, None, ALU.max)
                V.tensor_scalar(col[:, 1, :], c.degs[1][:, :], 1.0, None, ALU.max).then_inc(counts_ready, 1)
                v.wait_ge(roots_ready, 1)
                V.reciprocal(col[:, 0:2, :], col[:, 2:4, :])
                v.drain()
                V.scalar_tensor_tensor(out=norm_src[:, :], in0=out_degree[:, :], scalar=0.0, in1=col[:, 0, :],
                                       op0=ALU.is_gt, op1=ALU.mult)
                V.scalar_tensor_tensor(out=norm_dst[:, :], in0=c.degs[1][:, :], scalar=0.0, in1=col[:, 1, :],
                                       op0=ALU.is_gt, op1=ALU.mult)
                v.drain()
                V.tensor_tensor(work[:, :, :], h[:, :, :], spread(norm_src[:, :], [P, NB, D], 2), ALU.mult)
                v.drain()

            @block.scalar
            def _(act):
                act.wait_ge(counts_ready, 1)
                nc.scalar.activation(col[:, 2:4, :], col[:, 0:2, :], ACT.Sqrt).then_inc(roots_ready, 1)

        sum_neighbours(nc, top, z, c, "gcn1", work, res)

        def block_of(t):
            return lambda b, k: t[:, b, k * P:(k + 1) * P]

        def scale_bias(v, t, scale, bias, width):
            V, wide = nc.vector, [P, NB, width]
            if scale is not None:
                V.tensor_tensor(t[:, :, :], t[:, :, :], spread(scale[:, :], wide, 2), ALU.mult)
                v.drain()
            V.tensor_tensor(t[:, :, :], t[:, :, :], spread(bias[:, :], wide, 1), ALU.add)
            v.drain()

        def finish_first(v):
            scale_bias(v, hidden, norm_dst, b1, WIDE)
            nc.vector.tensor_scalar(hidden[:, :, :], hidden[:, :, :], 0.0, None, ALU.max)
            v.drain()
            nc.vector.tensor_tensor(hidden[:, :, :], hidden[:, :, :], spread(norm_src[:, :], [P, NB, WIDE], 2),
                                    ALU.mult)
            v.drain()

        project(nc, top, z, c, "gcn_w1", 1, WIDE, weights_in, arrived, block_of(res), lambda k: w1[:, :],
                hidden, finish_first)
        project(nc, top, z, c, "gcn_w2", 2, D, weights_in, arrived, block_of(hidden), lambda k: w2[:, k, :],
                work, lambda v: None)
        sum_neighbours(nc, top, z, c, "gcn2", work, res)

        with nc.Block() as block:
            @block.vector
            def _(v):
                scale_bias(v, res, norm_dst, b2, D)
                nc.vector.tensor_scalar(res[:, :, :], res[:, :, :], 0.0, None, ALU.max)
                v.drain()

        negative = hidden[:, :, 0:D]

        def finish_elu(v):
            scale_bias(v, work, None, fb1, D)
            nc.vector.tensor_scalar(negative, work[:, :, :], 0.0, None, ALU.min)
            v.drain()

        project(nc, top, z, c, "fc1_p", 1, D, weights_in, arrived, block_of(res), lambda k: fc1[:, :],
                work, finish_elu)
        with nc.Block() as block:
            @block.scalar
            def _(act):
                nc.scalar.activation(negative, negative, ACT.Exp).then_inc(exp_out, 1)

            @block.vector
            def _(v):
                V = nc.vector
                V.tensor_scalar(work[:, :, :], work[:, :, :], 0.0, -1.0, ALU.max, ALU.add)
                v.wait_ge(exp_out, 1)
                v.drain()
                V.tensor_tensor(work[:, :, :], work[:, :, :], negative, ALU.add)
                v.drain()

        def finish_out(v):
            scale_bias(v, res, None, fb2, D)
            nc.vector.tensor_tensor(x[:, :, :], x[:, :, :], res[:, :, :], ALU.add)
            v.drain()

        project(nc, top, z, c, "fc2_p", 1, D, weights_in, arrived, block_of(work), lambda k: fc2[:, :],
                res, finish_out)


def composed_attention(nc, top, z, c, a, x, h, res, work, out):
    NB = z.blocks
    with ExitStack() as ctx:
        def sb(name, shape, dt=F32):
            return ctx.enter_context(nc.sbuf_tensor(name, shape, dt))

        def sem(name):
            return top.sem(name)

        neigh_w = sb("neigh_w", [P, D])
        rel_land = sb("rel_land", [P, S, D])
        comp = sb("comp", [P, S, D])
        product = sb("l3_product", [P, S, D])
        total, part = sb("l3_total", [P, D]), sb("l3_sum", [P, D])
        scale, present = sb("l3_scale", [P, 1]), sb("l3_present", [P, NB])
        stream = Stream(nc, ctx, top, z, "l3", c.ells[1], c.plans[1], D, sources=2)
        soft = Softmax(nc, ctx, top, "l3", 1)
        weights_in, out_done = sem("l3_weights_in"), sem("out_done")
        tanh_out, final, x_out = sem("tanh_out"), sem("final"), sem("x_out")

        with nc.Block() as block:

            @block.sync
            def _(sp):
                sp.dma_start(neigh_w[:, :], a["neigh_w"]).then_inc(weights_in, 16)
                stream.load_all(sp, 0, 0)

            @block.gpsimd
            def _(pool):
                stream.open(pool, c.table, [stream.land, rel_land])
                scatter_rows(pool, z, c.perms[1], c.table, h, stream.table_in)
                pool.wait_ge(stream.table_in, z.stored)
                stream.gather_all(pool, 0, 0, [(c.table, 0, stream.land), (a["rel_emb"], 1, rel_land)])

            @block.scalar
            def _(act):
                all_bodies = stream.total(act)
                with act.Fori(0, all_bodies) as body:
                    soft.exponentials(act, body)

            @block.vector
            def _(v):
                V = nc.vector
                V.memset(comp[:, :, :], 0.0)
                v.drain()
                for k in range(HALVES):
                    v.sem_inc(stream.land_free[k], 1)
                V.tensor_scalar(present[:, :], c.degs[1][:, :], 0.0, None, ALU.is_gt)
                v.wait_ge(stream.table_in, z.stored)
                v.wait_ge(weights_in, 16)
                with v.Fori(0, NB) as b:
                    many, whole, first = stream.block(v, b)
                    second = stream.second(v, b)
                    soft.begin(c.degs[1][:, bass.ds(b, 1)])
                    V.memset(total[:, :], 0.0)
                    v.drain()

                    def compose(n, k):
                        half = slice(k * H, (k + 1) * H)
                        stream.wait(v, n, k)
                        V.tensor_tensor(comp[:, half, :], stream.land[:, half, :], rel_land[:, half, :], ALU.add)
                        v.drain()
                        v.sem_inc(stream.land_free[k], 1)

                    with v.Fori(0, many) as i:
                        n = first + i
                        soft.mark(c.iota_row)
                        compose(n, 0)
                        with v.If(i < whole):
                            compose(second + i, 1)
                        V.tensor_tensor(product[:, :, :], comp[:, :, :],
                                        h[:, bass.ds(b, 1), :].to_broadcast([P, S, D]), ALU.mult)
                        v.drain()
                        V.tensor_reduce(soft.score[:, :, :].rearrange("p s h -> p (s h)"),
                                        product[:, :, :], AX.X, ALU.add)
                        v.drain()
                        soft.scores(v)
                        soft.weigh(v, n, comp[:, :, :], product, total, part, D)
                        v.drain()
                    V.tensor_scalar(soft.denom[:, :], soft.denom[:, :], 1.0, None, ALU.max)
                    v.drain()
                    V.reciprocal(scale[:, :], soft.denom[:, :])
                    v.drain()
                    V.tensor_tensor(scale[:, :], scale[:, :], present[:, bass.ds(b, 1)], ALU.mult)
                    v.drain()
                    V.tensor_scalar(res[:, bass.ds(b, 1), :].rearrange("p a d -> p (a d)"), total[:, :],
                                    scale[:, 0:1], None, ALU.mult)
                    v.drain()

        project(nc, top, z, c, "neigh_p", 1, D, weights_in, 16,
                lambda b, _: res[:, b, :],
                lambda _: neigh_w[:, :], work, lambda v: None)
        with nc.Block() as block:
            @block.scalar
            def _(act):
                nc.scalar.activation(work[:, :, :], work[:, :, :], ACT.Tanh).then_inc(tanh_out, 1)

            @block.vector
            def _(v):
                v.wait_ge(tanh_out, 1)
                nc.vector.tensor_tensor(x[:, :, :], x[:, :, :], work[:, :, :], ALU.add).then_inc(final, 1)

            @block.gpsimd
            def _(pool):
                pool.wait_ge(final, 1)
                scatter_rows(pool, z, c.perms[1], c.table, x, x_out)

            @block.sync
            def _(sp):
                sp.wait_ge(x_out, z.stored)
                sp.dma_start(out[:, :], c.table[0:z.nodes, :]).then_inc(out_done, 16)
                sp.wait_ge(out_done, 16)


class Common:
    pass


def reorder(nc, top, z, name, source, to, x, of=None):
    out, back = top.sem(f"{name}_out"), top.sem(f"{name}_back")
    with nc.Block() as block:
        @block.gpsimd
        def _(pool):
            if of is not None:
                scatter_rows(pool, z, of, source, x, out)
                pool.wait_ge(out, z.stored)
            gather_rows(pool, z, to, source, x, back)
            pool.wait_ge(back, z.stored)


def program(nc, z, a, out):
    with ExitStack() as ctx:
        def sb(name, shape, dt=F32):
            return ctx.enter_context(nc.sbuf_tensor(name, shape, dt))

        def dram(name, shape, dt=F32):
            return nc.dram_tensor(name, shape, dt, kind="Internal").ap()

        NB = z.blocks
        iota_i = sb("iota_i", [P, P], I32)
        iota_ci = sb("iota_ci", [P, 1], I32)
        iota_row, iota_col, iota_rb = sb("iota_row", [P, P]), sb("iota_col", [P, 1]), sb("iota_rb", [P, P], BF16)
        before, zero = sb("before", [P, H, P], BF16), sb("zero", [P, D + 4])
        earlier = sb("earlier", [P, P])
        c = Common()
        c.iota_row = iota_row
        c.ident, c.ident_b = sb("ident", [P, P]), sb("ident_b", [P, P], BF16)
        c.natural_deg = sb("natural_deg", [P, 2, NB])
        c.degs = [sb(f"deg{q}", [P, NB]) for q in range(2)]
        c.plans = [sb(f"plan{q}", [P, 2 * NB + 2], I32) for q in range(2)]
        c.perms = [sb(f"perm{q}", [P, NB, 2], I32) for q in range(2)]
        c.ells = [dram(f"ell{q}", [(z.bodies + 2 * BLANKS) * S * P, 2], I32) for q in range(2)]
        c.perm_dram = [dram(f"perm_dram{q}", [z.rows, 2], I32) for q in range(2)]
        c.degree_dram = [dram(f"degree_dram{q}", [z.rows, 1]) for q in range(2)]
        c.order_dram = dram("order_dram", [z.rows, 1])
        c.table, c.table_w = dram("table", [z.rows + P, D]), dram("table_w", [z.rows + P, D + 4])
        consts_i = ctx.enter_context(nc.semaphore("consts_i"))
        consts_f = ctx.enter_context(nc.semaphore("consts_f"))
        blank_rows = ctx.enter_context(nc.semaphore("blank_rows"))

        with nc.Block() as block:
            @block.gpsimd
            def _(pool):
                nc.gpsimd.iota(iota_i[:, :], pattern=[[1, P]], base=0, channel_multiplier=0).then_inc(consts_i, 1)
                nc.gpsimd.iota(iota_ci[:, :], pattern=[[0, 1]], base=0, channel_multiplier=1).then_inc(consts_i, 1)

            @block.sync
            def _(sp):
                sp.wait_ge(consts_f, 1)
                sp.dma_start(c.table[z.rows:z.rows + P, :], zero[:, 0:D]).then_inc(blank_rows, 16)
                sp.dma_start(c.table_w[z.rows:z.rows + P, :], zero[:, :]).then_inc(blank_rows, 16)
                sp.wait_ge(blank_rows, 32)

            @block.vector
            def _(v):
                nc.vector.memset(zero[:, :], 0.0).then_inc(consts_f, 1)
                v.wait_ge(consts_i, 2)
                nc.vector.tensor_copy(iota_row[:, :], iota_i[:, :]).then_inc(consts_f, 1)
                nc.vector.tensor_copy(iota_rb[:, :], iota_i[:, :]).then_inc(consts_f, 1)
                nc.vector.tensor_copy(iota_col[:, :], iota_ci[:, :]).then_inc(consts_f, 1)
                v.wait_ge(consts_f, 4)
                nc.vector.tensor_scalar(earlier[:, :], iota_row[:, :], iota_col[:, 0:1], None, ALU.is_lt)
                nc.vector.tensor_scalar(c.ident[:, :], iota_row[:, :], iota_col[:, 0:1], None, ALU.is_equal)
                v.drain()
                nc.vector.tensor_scalar(before[:, :, :], spread(earlier[:, :], [P, H, P], 1),
                                        float(z.bits + 1), float(-2 * z.bits), ALU.mult, ALU.add)
                nc.vector.tensor_copy(c.ident_b[:, :], c.ident[:, :])
                v.drain()

        with Semaphores(nc) as top, ExitStack() as grouping:
            group_edges(nc, grouping, top, z, a, c, zero, (iota_row, iota_rb, iota_col, c.ident_b, before))

        x = sb("x", [P, NB, D])
        h, res, work = sb("h", [P, NB, D]), sb("res", [P, NB, D]), sb("work", [P, NB, D])
        col = sb("col", [P, 4, NB])
        with Semaphores(nc) as top:
            reorder(nc, top, z, "x0", a["x"], c.perms[0], x)
            normalize(nc, top, z, "n0", x, h, work, col)
        with Semaphores(nc) as top:
            attention_over_relations(nc, top, z, c, a, x, h, res, work)
        with Semaphores(nc) as top:
            reorder(nc, top, z, "x1", c.table, c.perms[1], x, of=c.perms[0])
            normalize(nc, top, z, "n1", x, h, work, col)
        with Semaphores(nc) as top:
            graph_attention(nc, top, z, c, a, x, h, res, work)
        with Semaphores(nc) as top:
            normalize(nc, top, z, "n2", x, h, work, col)
            graph_convolution(nc, top, z, c, a, x, h, res, work)
        with Semaphores(nc) as top:
            normalize(nc, top, z, "n3", x, h, work, col)
            composed_attention(nc, top, z, c, a, x, h, res, work, out)


NAMES = {"x": "x", "L0_gnn_edge_emb": "edge_emb", "L0_gnn_q_w": "q_w", "L0_gnn_k_w": "k_w", "L1_gnn_b": "gat_b",
         "L2_gnn_W1": "w1", "L2_gnn_b1": "b1", "L2_gnn_W2": "w2", "L2_gnn_b2": "b2", "L2_gnn_fc1_w": "fc1",
         "L2_gnn_fc1_b": "fb1", "L2_gnn_fc2_w": "fc2", "L2_gnn_fc2_b": "fb2", "L3_gnn_rel_emb": "rel_emb",
         "L3_gnn_neigh_w": "neigh_w"}


def kernel(**inputs):
    import numpy as _np
    import concourse.bacc as _bacc
    from concourse import mybir as _mybir
    from concourse.bass_utils import run_bass_kernel_spmd as _run

    nodes, edges = inputs["x"].shape[0], inputs["src"].shape[0]
    tiles_at_once = 2 * S * CHUNKS
    tiles = -(-edges // (P * tiles_at_once)) * tiles_at_once
    z = Shapes(nodes, tiles)
    fill = tiles * P - edges
    spare = (nodes + _np.arange(fill) % (z.rows - nodes)).astype(_np.int32)
    dummy, none = _np.full(fill, z.dummy, _np.int32), _np.zeros(fill, _np.int32)

    def padded(name, tail):
        return _np.concatenate([_np.asarray(inputs[name]), tail])

    arrays = {}
    for k, (key, other, kind) in enumerate((("src", "dst", "edge_type_64"), ("dst", "src", "edge_type_474"))):
        arrays[f"keys{k}"] = _np.ascontiguousarray(padded(key, spare).reshape(tiles, P).T)
        pair = _np.stack([padded(other, dummy), padded(kind, none)], axis=-1)
        arrays[f"payload{k}"] = _np.ascontiguousarray(pair.reshape(tiles, P, 2).transpose(1, 0, 2))
    for name, k in NAMES.items():
        arrays[k] = _np.ascontiguousarray(inputs[name])
    arrays["x"] = _np.concatenate([arrays["x"], _np.zeros((z.rows - nodes, D), _np.float32)])
    layers = inputs["L1_gnn_b"].shape[0]
    arrays["ws"], arrays["wd"] = (_np.ascontiguousarray(inputs[f"L1_gnn_W{k}"]) for k in "sd")
    arrays["att_s"], arrays["att_d"] = (_np.ascontiguousarray(inputs[f"L1_gnn_att_{k}"]).reshape(layers, D)
                                        for k in "sd")

    nc = _bacc.Bacc("TRN2", target_bir_lowering=False, num_devices=1)
    a = {k: nc.dram_tensor(f"in_{k}", v.shape, _mybir.dt.from_np(v.dtype), kind="ExternalInput").ap()
         for k, v in arrays.items()}
    a["gat_w"], a["gat_att"] = (a["ws"], a["wd"]), (a["att_s"], a["att_d"])
    a["key_cols"], a["payloads"] = (a["keys0"], a["keys1"]), (a["payload0"], a["payload1"])
    out = nc.dram_tensor("out_dram", (nodes, D), F32, kind="ExternalOutput").ap()
    program(nc, z, a, out)
    r = _run(nc, [{f"in_{k}": v for k, v in arrays.items()}], core_ids=[0])
    return r.results[0]["out_dram"]
```
